# Optimizing a Trainium2 kernel written in Bass

```python
import numpy as np
import jax
import jax.numpy as jnp

def _softmax(x, axis=-1):
    return jax.nn.softmax(x, axis=axis)

def _gelu(x):
    return jax.nn.gelu(x, approximate=True)

def _silu(x):
    return jax.nn.silu(x)

def _sigmoid(x):
    return jax.nn.sigmoid(x)

def _layernorm(x, axis=-1, eps=1e-05):
    m = jnp.mean(x, axis=axis, keepdims=True)
    v = jnp.var(x, axis=axis, keepdims=True)
    return (x - m) / jnp.sqrt(v + eps)

def _scatter_add(tgt, idx, src, axis=0):
    return tgt.at[idx].add(src)

def _segment_sum(src, seg, n):
    return jax.ops.segment_sum(src, seg, n)
kernel_name = 'mk_cond_seq_d2_seqx_r4_29cc88'

def setup_inputs(seed: int=0):
    np.random.seed(seed)
    _w = jnp.asarray

    def _rec_inputs():
        import jax
        import jax.numpy as jnp
        _rk = jax.random.key(seed)
        x = -0.0003482 + 1 * jax.random.normal(jax.random.fold_in(_rk, 1), (2, 1024, 288), jnp.float32)
        _lenS = 1024 - jax.random.randint(jax.random.fold_in(_rk, 7), (2,), 0, max(1, 1024 // 4) + 1, jnp.int32)
        _lenS2 = 1024 - jax.random.randint(jax.random.fold_in(_rk, 8), (2,), 0, max(1, 1024 // 4) + 1, jnp.int32)
        cond_1152 = 0.00257642 + 1.0011 * jax.random.normal(jax.random.fold_in(_rk, 11), (2, 288), jnp.float32)
        return (x, cond_1152)
    x, cond_1152 = _rec_inputs()

    def _L0_cond_setup():
        import jax, jax.numpy as jnp
        import numpy as np
        from jax.scipy.linalg import expm
        N, D, COND_DIM = (288, 64, 288)
        B, T = (16, 256)

        def _rotation(cond, W, b):
            v = jax.nn.silu(cond) @ W.T + b
            iu, ju = jnp.triu_indices(D, k=1)
            A = jnp.zeros((cond.shape[0], D, D), dtype=v.dtype)
            A = A.at[:, iu, ju].set(v).at[:, ju, iu].set(-v)
            return expm(A)
        key = jax.random.key(seed)
        k1, k2, k3, k4, k5 = jax.random.split(key, 5)
        x = jax.random.normal(k1, (B, T, N), dtype=jnp.float32)
        cond = jax.random.normal(k2, (B, COND_DIM), dtype=jnp.float32)
        P = jax.random.normal(k3, (N, D), dtype=jnp.float32)
        n_skew = D * (D - 1) // 2
        bound = 1.0 / np.sqrt(COND_DIM)
        W = jax.random.uniform(k4, (n_skew, COND_DIM), minval=-bound, maxval=bound, dtype=jnp.float32)
        b = jax.random.uniform(k5, (n_skew,), minval=-bound, maxval=bound, dtype=jnp.float32)
        return {'x': x, 'cond': cond, 'P': P, 'W': W, 'b': b}
    _L0_cond_all = _L0_cond_setup()
    _L0_cond_in = {k: v for k, v in _L0_cond_all.items() if k in ('P', 'W', 'b')}
    del _L0_cond_all

    def _L1_cond_setup():
        import jax, jax.numpy as jnp
        import numpy as np
        N, T, D, H = (32, 256, 288, 16)
        DH = D // H
        MLP = int(D * 4.0)
        EPS = 1e-06

        def _layernorm(x):
            m = jnp.mean(x, axis=-1, keepdims=True)
            v = jnp.var(x, axis=-1, keepdims=True)
            return (x - m) * jax.lax.rsqrt(v + EPS)

        def _modulate(x, shift, scale):
            return x * (1.0 + scale[:, None, :]) + shift[:, None, :]

        def _attention(x, qkv_w, qkv_b, proj_w, proj_b):
            n, t, d = x.shape
            scale = DH ** (-0.5)
            qkv = x @ qkv_w + qkv_b
            qkv = qkv.reshape(n, t, 3, H, DH)
            q, k, v = (qkv[:, :, 0], qkv[:, :, 1], qkv[:, :, 2])
            attn = jnp.einsum('nthd,ntkd->nthk', q * scale, k)
            attn = jax.nn.softmax(attn, axis=-1)
            out = jnp.einsum('nthk,ntkd->nthd', attn, v)
            out = out.transpose(0, 2, 1, 3).reshape(n, t, d)
            return out @ proj_w + proj_b

        def _mlp(x, fc1_w, fc1_b, fc2_w, fc2_b):
            h = jax.nn.gelu(x @ fc1_w + fc1_b, approximate=False)
            return h @ fc2_w + fc2_b
        key = jax.random.key(seed)
        ks = jax.random.split(key, 14)
        s = 0.02
        return {'x': jax.random.normal(ks[0], (N, T, D), jnp.float32), 'c': jax.random.normal(ks[1], (N, D), jnp.float32), 'qkv_w': jax.random.normal(ks[2], (D, 3 * D), jnp.float32) * s, 'qkv_b': jax.random.normal(ks[3], (3 * D,), jnp.float32) * s, 'proj_w': jax.random.normal(ks[4], (D, D), jnp.float32) * s, 'proj_b': jax.random.normal(ks[5], (D,), jnp.float32) * s, 'fc1_w': jax.random.normal(ks[6], (D, MLP), jnp.float32) * s, 'fc1_b': jax.random.normal(ks[7], (MLP,), jnp.float32) * s, 'fc2_w': jax.random.normal(ks[8], (MLP, D), jnp.float32) * s, 'fc2_b': jax.random.normal(ks[9], (D,), jnp.float32) * s, 'ada_w': jax.random.normal(ks[10], (D, 6 * D), jnp.float32) * s, 'ada_b': jax.random.normal(ks[11], (6 * D,), jnp.float32) * s}
    _L1_cond_all = _L1_cond_setup()
    _L1_cond_in = {k: v for k, v in _L1_cond_all.items() if k in ('qkv_w', 'qkv_b', 'proj_w', 'proj_b', 'fc1_w', 'fc1_b', 'fc2_w', 'fc2_b', 'ada_w', 'ada_b')}
    del _L1_cond_all
    return {'x': x, 'cond_1152': cond_1152, 'L0_cond_P': _L0_cond_in['P'], 'L0_cond_W': _L0_cond_in['W'], 'L0_cond_b': _L0_cond_in['b'], 'L1_cond_qkv_w': _L1_cond_in['qkv_w'], 'L1_cond_qkv_b': _L1_cond_in['qkv_b'], 'L1_cond_proj_w': _L1_cond_in['proj_w'], 'L1_cond_proj_b': _L1_cond_in['proj_b'], 'L1_cond_fc1_w': _L1_cond_in['fc1_w'], 'L1_cond_fc1_b': _L1_cond_in['fc1_b'], 'L1_cond_fc2_w': _L1_cond_in['fc2_w'], 'L1_cond_fc2_b': _L1_cond_in['fc2_b'], 'L1_cond_ada_w': _L1_cond_in['ada_w'], 'L1_cond_ada_b': _L1_cond_in['ada_b']}

def reference(x, cond_1152, L0_cond_P, L0_cond_W, L0_cond_b, L1_cond_qkv_w, L1_cond_qkv_b, L1_cond_proj_w, L1_cond_proj_b, L1_cond_fc1_w, L1_cond_fc1_b, L1_cond_fc2_w, L1_cond_fc2_b, L1_cond_ada_w, L1_cond_ada_b):
    import jax
    import jax.numpy as jnp

    def _L0_cond_ref(x, cond, P, W, b):
        import jax, jax.numpy as jnp
        import numpy as np
        from jax.scipy.linalg import expm
        N, D, COND_DIM = (288, 64, 288)
        B, T = (16, 256)

        def _rotation(cond, W, b):
            v = jax.nn.silu(cond) @ W.T + b
            iu, ju = jnp.triu_indices(D, k=1)
            A = jnp.zeros((cond.shape[0], D, D), dtype=v.dtype)
            A = A.at[:, iu, ju].set(v).at[:, ju, iu].set(-v)
            return expm(A)
        U, _ = jnp.linalg.qr(P)
        R = _rotation(cond, W, b)
        z = jnp.einsum('btn,nd->btd', x, U)
        z_rot = jnp.einsum('btd,bde->bte', z, R)
        x_rot = x + jnp.einsum('btd,nd->btn', z_rot - z, U)
        return x_rot

    def _L1_cond_ref(x, c, qkv_w, qkv_b, proj_w, proj_b, fc1_w, fc1_b, fc2_w, fc2_b, ada_w, ada_b):
        import jax, jax.numpy as jnp
        import numpy as np
        N, T, D, H = (32, 256, 288, 16)
        DH = D // H
        MLP = int(D * 4.0)
        EPS = 1e-06

        def _layernorm(x):
            m = jnp.mean(x, axis=-1, keepdims=True)
            v = jnp.var(x, axis=-1, keepdims=True)
            return (x - m) * jax.lax.rsqrt(v + EPS)

        def _modulate(x, shift, scale):
            return x * (1.0 + scale[:, None, :]) + shift[:, None, :]

        def _attention(x, qkv_w, qkv_b, proj_w, proj_b):
            n, t, d = x.shape
            scale = DH ** (-0.5)
            qkv = x @ qkv_w + qkv_b
            qkv = qkv.reshape(n, t, 3, H, DH)
            q, k, v = (qkv[:, :, 0], qkv[:, :, 1], qkv[:, :, 2])
            attn = jnp.einsum('nthd,ntkd->nthk', q * scale, k)
            attn = jax.nn.softmax(attn, axis=-1)
            out = jnp.einsum('nthk,ntkd->nthd', attn, v)
            out = out.transpose(0, 2, 1, 3).reshape(n, t, d)
            return out @ proj_w + proj_b

        def _mlp(x, fc1_w, fc1_b, fc2_w, fc2_b):
            h = jax.nn.gelu(x @ fc1_w + fc1_b, approximate=False)
            return h @ fc2_w + fc2_b
        ada = jax.nn.silu(c) @ ada_w + ada_b
        shift_msa, scale_msa, gate_msa, shift_mlp, scale_mlp, gate_mlp = jnp.split(ada, 6, axis=1)
        x = x + gate_msa[:, None, :] * _attention(_modulate(_layernorm(x), shift_msa, scale_msa), qkv_w, qkv_b, proj_w, proj_b)
        x = x + gate_mlp[:, None, :] * _mlp(_modulate(_layernorm(x), shift_mlp, scale_mlp), fc1_w, fc1_b, fc2_w, fc2_b)
        return x
    x = _L0_cond_ref(x, cond_1152, L0_cond_P, L0_cond_W, L0_cond_b)
    x = _L1_cond_ref(x, cond_1152, L1_cond_qkv_w, L1_cond_qkv_b, L1_cond_proj_w, L1_cond_proj_b, L1_cond_fc1_w, L1_cond_fc1_b, L1_cond_fc2_w, L1_cond_fc2_b, L1_cond_ada_w, L1_cond_ada_b)
    return x

_drawn_inputs = setup_inputs


def setup_inputs(seed=0):
    import zlib

    import numpy as np

    out = dict(_drawn_inputs(seed))
    spreads = {}
    factors = {'L1_cond_qkv_w': 8.0,
     'L1_cond_qkv_b': 8.0,
     'L1_cond_proj_w': 8.0,
     'L1_cond_proj_b': 22.1,
     'L1_cond_fc1_b': 64.0,
     'L1_cond_fc2_b': 23.03,
     'L1_cond_ada_b': 8.0,
     'L1_cond_fc1_w': 3.713,
     'L1_cond_fc2_w': 3.361}
    for name, (base, spread) in spreads.items():
        noise = np.random.default_rng([zlib.crc32(name.encode()), seed]).standard_normal(out[name].shape)
        drawn = base * np.exp(spread * noise) if base else spread * noise
        out[name] = jnp.asarray(drawn.astype(out[name].dtype))
    for name, factor in factors.items():
        out[name] = (out[name] * factor).astype(out[name].dtype)
    return out
```

```python
from contextlib import ExitStack

import concourse.bass as bass
from concourse import mybir

F32 = mybir.dt.float32
F16 = mybir.dt.float16
ALU = mybir.AluOpType
ACT = mybir.ActivationFunctionType
AX = mybir.AxisListType

B, T, D = 2, 1024, 288
R = 64
H, DH = 16, 18
MLP = 4 * D
P = 128
NT = B * T // P
CH = 512
NCH = B * T // CH
TPC = CH // P
BLK = ((0, 128), (128, 128), (256, 32))
NF = MLP // P
NSKEW = R * (R - 1) // 2
WROWS = 126
WTILES = NSKEW // WROWS
SQUARINGS = 16
FINE = 64.0
EPS = 1e-6


def build(nc, x, c, pmat, wskew, bskew, qkv_w, qkv_b, proj_w, proj_b, fc1_w, fc1_b, fc2_w, fc2_b, ada_w, ada_b, out):
    with ExitStack() as ctx:
        def sb(name, shape, dt=F32):
            return ctx.enter_context(nc.sbuf_tensor(name, shape, dt))

        def sem(name):
            return ctx.enter_context(nc.semaphore(name))

        psum = ctx.enter_context(nc.psum_tensor("psum", [P, 8, 512], F32))
        bank = [psum[:, i, :] for i in range(8)]

        X = sb("X", [P, NT, D])
        big = sb("big", [P, 22528])
        WL = big[0:WROWS, 0:WTILES * D].rearrange("p (t n) -> p t n", t=WTILES)
        o = WTILES * D
        WT = big[:, o:o + 3 * (NSKEW + 1)].rearrange("p (b n) -> p b n", b=3)
        o += 3 * (NSKEW + 1)
        ADA = big[:, o:o + 18 * D].rearrange("p (b n) -> p b n", b=3)
        XT = big[:, 22528 - 3 * B * T:22528].rearrange("p (b t) -> p b t", b=3)
        stage = sb("stage", [P, 18 * D])
        SWQ = stage[:, 0:9 * D].rearrange("p (b n) -> p b n", b=3)
        SW2 = stage[:, 9 * D:18 * D].rearrange("p (b n) -> p b n", b=NF)
        SWP = big[:, 0:3 * D].rearrange("p (b n) -> p b n", b=3)
        SW1 = big[:, 3 * D:15 * D].rearrange("p (b n) -> p b n", b=3)
        WQ = sb("WQ", [P, 5, 3 * D], F16)
        WP = sb("WP", [P, 5, D], F16)
        W1 = sb("W1", [P, 5, MLP], F16)
        W2 = sb("W2", [P, 2, NF, D], F16)
        SB2 = big[0:1, 15 * D:16 * D]
        B2 = sb("B2", [1, 2, D], F16)
        GATE = sb("GATE", [P, 2, B, D])
        MOD = sb("MOD", [P, 4, 3, B])
        ident = sb("ident", [P, P])
        ones = sb("ones", [P, P])

        scratch = sb("scratch", [P, 9320])
        used = [0]

        def part(rows, *dims):
            n = 1
            for d in dims:
                n *= d
            a = scratch[0:rows, used[0]:used[0] + n]
            used[0] += n
            if len(dims) == 2:
                a = a.rearrange("p (a b) -> p a b", a=dims[0])
            if len(dims) == 3:
                a = a.rearrange("p (a b c) -> p a b c", a=dims[0], b=dims[1])
            return a

        ZT = part(R, B * T)
        ROW = part(1, NSKEW + 1)
        ADAB = part(1, 6 * D)
        ROT = part(R, B, D)
        below = part(R, R)
        lowrow = sb("lowrow", [P, 1])
        TWO = part(P, P)
        MI = part(P, 3, P)
        PS = part(P, 3, R)
        PT2 = part(P, D)
        CT = part(P, 3, B)
        SC = part(P, 4, 3, B)
        sc = SC[:, 3]
        G = part(R, 2 * R)
        A = part(R, R)
        RI = part(R, R)
        HALF = part(R, R)
        RHO = part(R, R)
        ROWS = part(R, 4, R)
        CG = part(R, R)
        CA = part(R, R)
        RA = part(R, R)
        TR = part(R, 2, R)
        dg = part(R, 8)
        V2 = part(P, R)
        LT = part(R, B, R)
        LM = part(R, B, R)
        NEGI = part(R, R)
        XX = part(P, 2 * R)
        YY = part(P, 2, 2 * R)
        T1 = part(P, R)
        NTs = part(P, R)

        ST = sb("ST", [P, 2, 8, NT])
        MV = sb("MV", [P, 2, NT, 2])
        BN = sb("BN", [P, 2, 6])
        FOUR = sb("FOUR", [1, P], F16)
        SELV = sb("SELV", [P, DH], F16)
        MX = sb("MX", [P, NCH, 64])
        MR = sb("MR", [P, NCH, 64], F16)
        RD = sb("RD", [P, 2, 16])
        VG = sb("VG", [P, 2, 16, DH + 1])
        o = 0
        DX = D + 64
        XN = scratch[:, o:o + 2 * TPC * DX].rearrange("p (a t n) -> p a t n", a=2, t=TPC)
        o += 2 * TPC * DX
        T32 = scratch[:, o:o + 2 * CH].rearrange("p (a n) -> p a n", a=2)
        o += 2 * CH
        HT = scratch[:, o:o + 5 * CH].bitcast(F16).rearrange("p (a s n) -> p a s n", a=2, s=5)
        o += 5 * CH
        QS = scratch[:, o:o + 4 * CH].bitcast(F16).rearrange("p (a s n) -> p a s n", a=4, s=2)
        assert o + 4 * CH <= 9320
        QKT = [big[:, 14336:22528].bitcast(F16).rearrange("p (w c) -> p w c", w=2),
               big[:, 0:8192].bitcast(F16).rearrange("p (w c) -> p w c", w=2)]
        VT = big[:, 8192:12288].bitcast(F16)
        E = big[:, 12288:12288 + 3 * CH].rearrange("p (a n) -> p a n", a=3)
        CST = big[:, 12288 + 3 * CH:14336].bitcast(F16)
        MASKQ, MASKK = CST[0:8, 0:CH], CST[0:9, CH:2 * CH]
        AO = stage[:, 0:NT * D].rearrange("p (b a e c d) -> p b a e c d", b=B, a=8, e=2, c=8)
        GT = [big[:, 0:NF * CH].bitcast(F16).rearrange("p (s f n) -> p s f n", s=2, f=NF),
              big[:, NF * CH:2 * NF * CH].bitcast(F16).rearrange("p (s f n) -> p s f n", s=2, f=NF)]
        G32 = big[:, 2 * NF * CH:2 * NF * CH + 2 * CH].rearrange("p (a n) -> p a n", a=2)
        YT = big[:, 2 * (NF + 1) * CH:2 * (NF + 1) * CH + 6 * D].rearrange("p (a n) -> p a n", a=6)
        qkd = nc.dram_tensor("qkv_halves", [2, NCH, 3 * D, CH], F16, kind="Internal").ap()

        in_p, in_c, in_w, in_row, in_ada, in_adab, in_wt = (sem(n) for n in ("in_p", "in_c", "in_w", "in_row", "in_ada", "in_adab", "in_wt"))
        in_x = [sem(f"in_x{i}") for i in range(NCH)]
        consts = sem("consts")
        pool_step = sem("pool_step")
        ct_clear = sem("ct_clear")
        silu_e = sem("silu_e")
        silu = sem("silu")
        gram = sem("gram")
        state0 = sem("state0")
        piv_row, piv_inv, gcoef, g_new = sem("piv_row"), sem("piv_inv"), sem("gcoef"), sem("g_new")
        rho_ready, row_ready = sem("rho_ready"), sem("row_ready")
        a_row, a_sum, a_piv, acoef, a_new, a_sign = sem("a_row"), sem("a_sum"), sem("a_piv"), sem("acoef"), sem("a_new"), sem("a_sign")
        fill_ready, fill_done = sem("fill_ready"), sem("fill_done")
        skew_raw, skew_sb, skew_low, skew_psum, skew_ready = sem("skew_raw"), sem("skew_sb"), sem("skew_low"), sem("skew_psum"), sem("skew_ready")
        exp_psum, exp_sb = sem("exp_psum"), sem("exp_sb")
        diag, root, basis = sem("diag"), sem("root"), sem("basis")
        rot_psum, rot_sb = sem("rot_psum"), sem("rot_sb")
        delta_ready, x_rot = sem("delta_ready"), sem("x_rot")
        weights = sem("weights")
        mod_part = sem("mod_part")
        bn_s, stats, root2, scales = sem("bn_s"), sem("stats"), sem("root2"), sem("scales")
        ht_ones = sem("ht_ones")
        xn_ready, tr_ready, t32_ready, cast_done, split_done = (
            sem(n) for n in ("xn_ready", "tr_ready", "t32_ready", "cast_done", "split_done"))
        qk_ready, qk_high, qk_low = sem("qk_ready"), sem("qk_high"), sem("qk_low")
        qk_out = [sem(f"qk_out{i}") for i in range(4)]
        att_const = sem("att_const")
        att_rows = [sem(f"att_rows{i}") for i in range(2)]
        qk_in = [sem(f"qk_in{i}") for i in range(NCH)]
        v_in = [sem(f"v_in{i}") for i in range(NCH)]
        max_in = [sem(f"max_in{i}") for i in range(NCH)]
        mx_ready, mx_used, mx_half = sem("mx_ready"), sem("mx_used"), sem("mx_half")
        s_ready, exp_done = sem("s_ready"), sem("exp_done")
        vg_psum, vg_ready, pv_ready, o_sum, o_norm = (sem(n) for n in ("vg_psum", "vg_ready", "pv_ready", "o_sum", "o_norm"))
        proj_ready, proj_mul, x_mid = sem("proj_ready"), sem("proj_mul"), sem("x_mid")
        fc1_ready, gelu_sb, g_high, g_low = sem("fc1_ready"), sem("gelu_sb"), sem("g_high"), sem("g_low")
        fc2_ready, y_mul, y_ready = sem("fc2_ready"), sem("y_mul"), sem("y_ready")
        y_out = [sem(f"y_out{i}") for i in range(6)]
        xn_main = sem("xn_main")

        PIV = [bank[0], bank[1]]
        AROW = bank[2]
        FILL = [bank[3], bank[4]]
        SKEW = bank[5]
        EXPM = bank[6]
        MISC = bank[7]

        FPT, FW, FX, FZ, FG, FM = 0, 1, 13, 25, 29, 33
        NFILL = 34
        fill_step = {1: [0]}
        for n in range(12):
            fill_step.setdefault(2 + n, []).append(FW + n)
            fill_step.setdefault(20 + n, []).append(FX + n)
        for n in range(4):
            fill_step.setdefault(36 + 4 * n, []).append(FZ + n)
            fill_step.setdefault(53 + 2 * n, []).append(FG + n)
        fill_step.setdefault(61, []).append(FM)
        SKEW_AT = 15
        EXP_AT = SKEW_AT + R // 4 + 1
        NEXP = 4 + SQUARINGS
        LAG = 2

        TRB = [bank[0], bank[1]]
        QB = [bank[2], bank[3]]
        MXB, SB, VB, PO = [bank[0], bank[1]], [bank[2], bank[3]], bank[4], [bank[5], bank[6]]
        FB = [bank[2], bank[3], bank[4]]
        YB = [bank[5], bank[6]]
        PARTS = ((0, 0, P), (1, 1, P), (2, 0, P), (3, 1, P), (0, 2, P), (1, 3, P), (4, 4, 98))
        MT = [(126 * m, min(126, 3 * D - 126 * m)) for m in range(7)]
        NQ = len(MT)
        UNITS = 16 * NCH
        QSCALE = 8.0
        MROW = 16.0
        MASK = (240.0, -60000.0)
        HALVES = 3 * DH
        MROWS = HALVES + 8
        LEAD = 22
        BEHIND = 2

        def operand(n, w, u, g, rows):
            r = R * (n % 2)
            return QKT[n // 2][r:r + rows, w, 4 * u + g:4 * u + g + 64 * P - 63:64]

        block = ctx.enter_context(nc.Block())

        @block.sync
        def _(sp):
            for b, (r0, n) in enumerate(BLK):
                sp.dma_start(PS[0:n, b, :], pmat[r0:r0 + n, :]).then_inc(in_p, 16)
            sp.wait_ge(ct_clear, 1)
            for b, (r0, n) in enumerate(BLK):
                sp.dma_start(CT[0:n, b, :], c[:, r0:r0 + n].rearrange("b p -> p b"), allow_slow_non_contiguous=True).then_inc(in_c, 16)
            sp.dma_start(WL, wskew.rearrange("(t p) n -> p t n", p=WROWS)).then_inc(in_w, 16)
            sp.dma_start(ROW[:, 1:], bskew.rearrange("(a n) -> a n", a=1)).then_inc(in_row, 16)
            for i in range(NCH):
                b, a = divmod(TPC * i, 8)
                sp.dma_start(X[:, TPC * i:TPC * i + TPC, :], x[b].rearrange("(p a) d -> p a d", a=8)[:, a:a + TPC, :]).then_inc(in_x[i], 16)
            sp.dma_start(ADAB[:, :], ada_b.rearrange("(a n) -> a n", a=1)).then_inc(in_adab, 16)
            for b, (r0, n) in enumerate(BLK):
                sp.dma_start(ADA[0:n, b, :], ada_w[r0:r0 + n, :]).then_inc(in_ada, 16)
            for w, bias, dst in ((qkv_w, qkv_b, SWQ), (proj_w, proj_b, SWP), (fc1_w, fc1_b, SW1)):
                if w is proj_w:
                    sp.wait_ge(fill_done, FX)
                sp.dma_start(dst[:, 0:2, :], w[0:2 * P, :].rearrange("(b p) n -> p b n", p=P)).then_inc(in_wt, 16)
                for g in range(3):
                    sp.dma_start(dst[32 * g:32 * g + 32, 2, :], w[2 * P:D, :]).then_inc(in_wt, 16)
                for g in range(2):
                    sp.dma_start(dst[96 + g:97 + g, 2, :], bias.rearrange("(a n) -> a n", a=1)).then_inc(in_wt, 16)
            sp.dma_start(SW2, fc2_w.rearrange("(b p) n -> p b n", p=P)).then_inc(in_wt, 16)
            sp.dma_start(SB2[:, :], fc2_b.rearrange("(a n) -> a n", a=1)).then_inc(in_wt, 16)
            def halves_out(n):
                for m, (f0, k) in enumerate(MT):
                    idx = NQ * n + m
                    sp.wait_ge(qk_low, idx + 1)
                    sp.dma_start(qkd[:, n, f0:f0 + k, :].rearrange("c f n -> f c n"), QS[0:k, idx % 4, :, :]).then_inc(qk_out[idx % 4], 16)
                for j in range(4):
                    sp.wait_ge(qk_out[j], 16 * len(range(j, NQ * (n + 1), 4)))

            def rows_in(dst, r, n, half, w, s_):
                sp.dma_start(dst[r:r + DH, :].rearrange("p (h c) -> p h c", h=H),
                             qkd[half, n, D * w:D * w + D, :].rearrange("(h d) c -> d h c", h=H)).then_inc(s_, 16)

            def qk_rows(n):
                for w, halves in ((0, (0, 1, 0)), (1, (0, 0, 1))):
                    for c_, half in enumerate(halves):
                        rows_in(QKT[n // 2][:, w, :], R * (n % 2) + DH * c_, n, half, w, qk_in[n])

            def v_rows(n):
                for half in range(2):
                    rows_in(VT, R * (n % 2) + DH * half, n, half, 2, v_in[n])

            def const_rows(n):
                r = R * (n % 2) + HALVES
                for w, k, src in ((0, 8, MASKQ), (1, 9, MASKK)):
                    sp.dma_start(QKT[n // 2][r:r + k, w, :].rearrange("p (h c) -> p h c", h=H),
                                 src.unsqueeze(1).broadcast_to([k, H, CH])).then_inc(att_rows[n // 2], 16)

            def max_row(n):
                sp.wait_ge(mx_half, n + 1)
                r = R * (n % 2) + MROWS
                sp.dma_start(QKT[n // 2][r:r + 1, 0, :].rearrange("p (j u) -> p j u", j=P), MR[:, n, :]).then_inc(max_in[n], 16)

            sp.wait_ge(att_const, 1)
            sp.wait_ge(fill_done, NFILL)
            const_rows(0)
            const_rows(1)
            halves_out(0)
            qk_rows(0)
            v_rows(0)
            halves_out(1)
            qk_rows(1)
            v_rows(1)
            sp.wait_ge(weights, 6)
            const_rows(2)
            const_rows(3)
            halves_out(2)
            qk_rows(2)
            halves_out(3)
            qk_rows(3)
            max_row(0)
            sp.wait_ge(vg_psum, 4)
            v_rows(2)
            max_row(1)
            sp.wait_ge(vg_psum, 8)
            v_rows(3)
            max_row(2)
            max_row(3)

            for t in range(NT):
                sp.wait_ge(y_ready, t + 1)
                sp.dma_start(out[t // 8].rearrange("(p a) d -> p a d", a=8)[:, t % 8, :], YT[:, t % 6, :]).then_inc(y_out[t % 6], 16)
            for j in range(6):
                sp.wait_ge(y_out[j], 16 * len(range(j, NT, 6)))

        N_WT = 16 * (3 * 6 + 2)

        @block.gpsimd
        def _(pool):
            steps = [0]

            def chain(ins):
                steps[0] += 1
                ins.then_inc(pool_step, 1)
                pool.wait_ge(pool_step, steps[0])

            pool.memset(CT[:, :, :], 0.0).then_inc(ct_clear, 1)
            chain(pool.memset(ident[:, :], 0.0))
            chain(pool.memset(below[:, :], -1.0))
            chain(pool.affine_select(out=ident[:, :], in_=ident[:, :], compare_op=ALU.not_equal, fill=1.0, base=0,
                                     pattern=[[-1, P]], channel_multiplier=1))
            chain(pool.affine_select(out=below[:, :], in_=below[:, :], compare_op=ALU.is_gt, fill=0.0, base=0,
                                     pattern=[[-1, R]], channel_multiplier=1))
            chain(pool.memset(WT[:, :, 0:1], 0.0))
            chain(pool.memset(ROW[:, 0:1], 0.0))
            chain(pool.memset(ones[:, :], 1.0))
            pool.tensor_copy(G[:, R:2 * R], ident[0:R, 0:R]).then_inc(consts, 1)
            pool.wait_ge(consts, 1)
            chain(pool.tensor_scalar(TWO[:, :], ident[:, :], 2.0, None, ALU.mult))
            chain(pool.tensor_scalar(NEGI[:, :], ident[0:R, 0:R], -1.0, None, ALU.mult))
            for m in range(3):
                for g in range(2):
                    for h in range(2):
                        chain(pool.tensor_scalar(MI[R * g:R * g + R, m, R * h:R * h + R],
                                                 ident[R * g:R * g + R, R * g:R * g + R], 4.0 - m, None, ALU.mult))
            pool.memset(MOD[:, :, :, :], 0.0).then_inc(consts, 1)
            pool.wait_ge(consts, 2)
            chain(pool.memset(lowrow[:, :], 0.0))
            chain(pool.memset(lowrow[64:P, :], -1.0))
            chain(pool.affine_select(out=lowrow[96:P, :], in_=lowrow[96:P, :], compare_op=ALU.not_equal, fill=0.0, base=0,
                                     pattern=[[0, 1]], channel_multiplier=1))
            chain(pool.tensor_copy(SELV[:, :], ident[:, 0:DH]))
            for j in (DH, R, R + DH):
                chain(pool.tensor_tensor(SELV[:, :], SELV[:, :], ident[:, j:j + DH], ALU.add))
            chain(pool.memset(VG[:, :, :, DH:DH + 1], 1.0))
            chain(pool.memset(FOUR[:, :], FINE))
            pool.wait_ge(skew_sb, 2)
            for b in range(B):
                pool.affine_select(out=LM[:, b, :], in_=LT[:, b, :], compare_op=ALU.is_gt, fill=0.0, base=0,
                                   pattern=[[-1, R]], channel_multiplier=1).then_inc(skew_low, 1)
            pool.wait_ge(in_wt, N_WT)
            for src, dst, n in ((SWQ, WQ, 3 * D), (SWP, WP, D), (SW1, W1, MLP)):
                chain(pool.tensor_scalar(src[:, 0:2, :], src[:, 0:2, :], FINE, None, ALU.mult))
                chain(pool.tensor_copy(dst[:, 0:2, :], src[:, 0:2, :]))
                pool.tensor_tensor(dst[:, 2:4, :], src[:, 0:2, :], dst[:, 0:2, :], ALU.subtract).then_inc(weights, 1)
                r = slice(0, 98)
                chain(pool.tensor_scalar(src[r, 2, :], src[r, 2, :], FINE, None, ALU.mult))
                chain(pool.tensor_copy(dst[r, 4, :], src[r, 2, :]))
                chain(pool.tensor_scalar(dst[r, 4, :], dst[r, 4, :], lowrow[r, :], None, ALU.mult))
                pool.tensor_tensor(dst[r, 4, :], src[r, 2, :], dst[r, 4, :], ALU.add).then_inc(weights, 1)
            chain(pool.tensor_scalar(SW2, SW2, FINE, None, ALU.mult))
            chain(pool.tensor_copy(W2[:, 0], SW2))
            pool.tensor_tensor(W2[:, 1], SW2, W2[:, 0], ALU.subtract).then_inc(weights, 1)
            chain(pool.tensor_scalar(SB2[:, :], SB2[:, :], FINE, None, ALU.mult))
            chain(pool.tensor_copy(B2[:, 0], SB2[:, :]))
            pool.tensor_tensor(B2[:, 1], SB2[:, :], B2[:, 0], ALU.subtract).then_inc(weights, 1)
            pool.wait_ge(fill_done, NFILL)
            chain(pool.memset(MASKK, MROW))
            for dst, value, keep in ((MASKQ, MASK[0], ALU.is_equal), (MASKK[0:8], MASK[1], ALU.not_equal)):
                chain(pool.memset(dst, value))
                sel = pool.affine_select(out=dst.rearrange("p (m c) -> p m c", m=8), in_=dst.rearrange("p (m c) -> p m c", m=8),
                                         compare_op=keep, fill=0.0, base=0, pattern=[[-1, 8], [0, 64]], channel_multiplier=1)
                chain(sel) if dst is MASKQ else sel.then_inc(att_const, 1)

        @block.tensor
        def _(pe):
            pe.wait_ge(consts, 1)
            pe.wait_ge(in_p, 48)
            for b, (r0, n) in enumerate(BLK):
                mm = pe.matmul(MISC[0:R, 0:R], PS[0:n, b, :], PS[0:n, b, :], start=(b == 0), stop=(b == 2))
            mm.then_inc(gram, 1)

            def filler(n):
                if n >= 2:
                    pe.wait_ge(fill_done, n - 1)
                f = FILL[n % 2]
                if n == FPT:
                    for g in range(2):
                        for b, (r0, k) in enumerate(BLK):
                            mm = pe.matmul(f[R * g:R * g + R, r0:r0 + k], PS[0:k, b, :], ident[0:k, 0:k], start=True, stop=True)
                elif n < FX:
                    q, b = divmod(n - FW, 3)
                    if n == FW:
                        pe.wait_ge(in_w, 16)
                    r0, k = BLK[b]
                    for j in range(4):
                        mm = pe.transpose(f[0:k, WROWS * j:WROWS * j + WROWS], WL[:, 4 * q + j, r0:r0 + k], ident[0:WROWS, 0:WROWS])
                elif n < FZ:
                    i, b = divmod(n - FX, 3)
                    if b == 0:
                        pe.wait_ge(in_x[i], 16)
                    r0, k = BLK[b]
                    for j in range(TPC):
                        mm = pe.transpose(f[0:k, P * j:P * j + P], X[:, TPC * i + j, r0:r0 + k], ident[:, :])
                elif n < FG:
                    i = n - FZ
                    pe.wait_ge(fill_done, FX + 3 * i + 3)
                    for b, (r0, k) in enumerate(BLK):
                        mm = pe.matmul(f[0:R, :], PS[0:k, b, :], XT[0:k, b, CH * i:CH * i + CH], start=(b == 0), stop=(b == 2))
                elif n < FM:
                    g, b = divmod(n - FG, 2)
                    if n == FG:
                        pe.wait_ge(in_ada, 48)
                        pe.wait_ge(in_adab, 16)
                        pe.wait_ge(silu, 1)
                    cols = slice((2 + 3 * g) * D, (3 + 3 * g) * D)
                    for kb, (r0, k) in enumerate(BLK):
                        pe.matmul(f[:, 0:D], sc[0:k, kb, b:b + 1].broadcast_to([k, P]), ADA[0:k, kb, cols], start=(kb == 0), stop=False)
                    mm = pe.matmul(f[:, 0:D], ones[0:1, :], ADAB[:, cols], start=False, stop=True)
                else:
                    for v, vec in enumerate((0, 1, 3, 4)):
                        for mb, (c0, m) in enumerate(BLK):
                            for rep in range(3 if mb == 2 else 1):
                                o_ = f[32 * rep:32 * rep + m, (v * 3 + mb) * B:(v * 3 + mb) * B + B]
                                cols = slice(vec * D + c0, vec * D + c0 + m)
                                for kb, (r0, k) in enumerate(BLK):
                                    pe.matmul(o_, ADA[0:k, kb, cols], sc[0:k, kb, :], start=(kb == 0), stop=False)
                                mm = pe.matmul(o_, ADAB[:, cols], ones[0:1, 0:B], start=False, stop=True)
                mm.then_inc(fill_ready, 1)

            def skew_rows(q):
                if q == 0:
                    pe.wait_ge(fill_done, FX)
                    pe.wait_ge(silu, 1)
                    pe.wait_ge(in_row, 16)
                for i in range(4 * q, 4 * q + 4):
                    at = i * (2 * R - 1 - i) // 2 - i
                    o_ = SKEW[0:R, B * i:B * i + B]
                    for kb, (r0, k) in enumerate(BLK):
                        pe.matmul(o_, WT[0:k, kb, at:at + R], sc[0:k, kb, :], start=(kb == 0), stop=False)
                    mm = pe.matmul(o_, ROW[:, at:at + R], ones[0:1, 0:B], start=False, stop=True)
                if q == R // 4 - 1:
                    mm.then_inc(skew_raw, 1)

            def skew_matrix():
                pe.wait_ge(consts, 2)
                pe.wait_ge(skew_low, 2)
                for b in range(B):
                    o_ = EXPM[R * b:R * b + R, 0:R]
                    pe.matmul(o_, LM[:, b, :], ident[0:R, 0:R], start=True, stop=False)
                    mm = pe.matmul(o_, NEGI[:, :], LM[:, b, :], start=False, stop=True)
                mm.then_inc(skew_psum, 1)

            def exp_step(n):
                if n == 0:
                    pe.wait_ge(consts, 2)
                    pe.wait_ge(skew_ready, 2)
                else:
                    pe.wait_ge(exp_sb, n)
                src = YY[:, (n + 1) % 2, :]
                for b in range(B):
                    g = slice(R * b, R * b + R)
                    for h in range(2):
                        cols = slice(R * h, R * h + R)
                        if n < 3:
                            pe.matmul(EXPM[g, cols], ident[g, g], MI[g, n, cols], start=True, stop=False)
                        elif n >= 4:
                            pe.matmul(EXPM[g, cols], TWO[g, g], src[g, cols], start=True, stop=False)
                        lhs = (XX if n < 4 else src)[g, R - R * h:2 * R - R * h]
                        rhs = ident[g, g] if n == 0 else src[g, cols]
                        mm = pe.matmul(EXPM[g, cols], lhs, rhs, start=(n == 3), stop=True)
                mm.then_inc(exp_psum, 1)

            for k in range(R + LAG):
                if k < R:
                    pe.wait_ge(g_new, k + 1)
                    if k >= 2:
                        pe.wait_ge(row_ready, k - 1)
                    pe.matmul(PIV[k % 2][0:R, k:R + k + 1], ident[0:R, k:k + 1].broadcast_to([R, R]), G[:, k:R + k + 1],
                              start=True, stop=True).then_inc(piv_row, 1)
                j = k - LAG
                if j >= 0:
                    pe.wait_ge(a_new, j + 1)
                    pe.matmul(AROW[0:R, j:R], ident[0:R, j:j + 1].broadcast_to([R, R]), A[:, j:R],
                              start=True, stop=True).then_inc(a_row, 1)
                for n in fill_step.get(k, ()):
                    filler(n)
                if SKEW_AT <= k < SKEW_AT + R // 4:
                    skew_rows(k - SKEW_AT)
                if k == EXP_AT:
                    skew_matrix()
                if EXP_AT < k <= EXP_AT + NEXP:
                    exp_step(k - EXP_AT - 1)

            pe.wait_ge(basis, 2)
            pe.wait_ge(exp_sb, NEXP)
            last = YY[:, (NEXP + 1) % 2, :]
            for b in range(B):
                g = slice(R * b, R * b + R)
                mm = pe.matmul(EXPM[g, 0:R], last[g, R:2 * R], V2[g, :], start=True, stop=True)
            mm.then_inc(rot_psum, 1)
            pe.wait_ge(rot_sb, 1)
            for b in range(B):
                g = slice(R * b, R * b + R)
                mm = pe.matmul(SKEW[g, 0:R], T1[g, :], V2[g, :], start=True, stop=True)
            mm.then_inc(rot_psum, 1)
            pe.wait_ge(rot_sb, 2)
            for b in range(B):
                g = slice(R * b, R * b + R)
                mm = pe.matmul(PIV[b][0:R, 0:D], NTs[g, :], PT2[g, :], start=True, stop=True)
            mm.then_inc(rot_psum, 1)
            pe.wait_ge(rot_sb, 4)
            pe.wait_ge(fill_done, NFILL)
            for t in range(NT):
                if t >= 2:
                    pe.wait_ge(x_rot, t - 1)
                pe.matmul(FILL[t % 2][:, 0:D], ZT[:, P * t:P * t + P], ROT[:, t // 8, :], start=True, stop=True).then_inc(delta_ready, 1)

            def turn(n):
                pe.wait_ge(xn_ready, n + 1)
                for b, (r0, k) in enumerate(BLK):
                    if 3 * n + b >= 2:
                        pe.wait_ge(t32_ready, 3 * n + b - 1)
                    f = TRB[(3 * n + b) % 2]
                    for j in range(TPC):
                        rows = 96 if b == 2 else P
                        mm = pe.transpose(f[0:rows, P * j:P * j + P], XN[:, n % 2, j, r0:r0 + rows], ident[:, :])
                    mm.then_inc(tr_ready, 1)

            def qkv(n):
                pe.wait_ge(split_done, 3 * n + 3)
                if n == 0:
                    pe.wait_ge(weights, 2)
                for m, (f0, k) in enumerate(MT):
                    idx = NQ * n + m
                    if idx >= 2:
                        pe.wait_ge(qk_low, idx - 1)
                    for p_, (a_, w_, r) in enumerate(PARTS):
                        mm = pe.matmul(QB[idx % 2][0:k, :], WQ[0:r, w_, f0:f0 + k], HT[0:r, n % 2, a_, :], start=(p_ == 0), stop=(p_ == 6))
                    mm.then_inc(qk_ready, 1)

            turn(0)
            for n in range(NCH):
                if n + 1 < NCH:
                    turn(n + 1)
                qkv(n)

            def maxima(s_):
                n, u = divmod(s_, 16)
                if u == 0:
                    pe.wait_ge(qk_in[n], 96)
                    pe.wait_ge(att_rows[n // 2], 64)
                if s_ >= 2:
                    pe.wait_ge(mx_used, s_ - 1)
                for g in range(4):
                    mm = pe.matmul(MXB[s_ % 2][:, P * g:P * g + P], operand(n, 0, u, g, MROWS), operand(n, 1, u, g, MROWS),
                                   start=True, stop=True)
                mm.then_inc(mx_ready, 1)

            def scores(s_):
                n, u = divmod(s_, 16)
                if u == 0:
                    pe.wait_ge(max_in[n], 16)
                if s_ >= 2:
                    pe.wait_ge(exp_done, s_ - 1)
                for g in range(4):
                    mm = pe.matmul(SB[s_ % 2][:, P * g:P * g + P], operand(n, 1, u, g, MROWS + 1), operand(n, 0, u, g, MROWS + 1),
                                   start=True, stop=True)
                mm.then_inc(s_ready, 1)

            def v_groups(w):
                n, q = divmod(w, 4)
                r = R * (n % 2)
                if q == 0:
                    pe.wait_ge(v_in[n], 32)
                if w:
                    pe.wait_ge(vg_ready, w)
                for g in range(16):
                    mm = pe.matmul(VB[:, DH * g:DH * g + DH], VT[r:r + 2 * DH, 16 * q + g:16 * q + g + 64 * P - 63:64], SELV[r:r + 2 * DH, :],
                                   start=True, stop=True)
                mm.then_inc(vg_psum, 1)

            def values(s_):
                w, q = divmod(s_, 4)
                pe.wait_ge(exp_done, s_ + 1)
                if q == 0:
                    pe.wait_ge(vg_ready, w + 1)
                    if w >= 2:
                        pe.wait_ge(o_norm, w - 1)
                for g in range(4):
                    mm = pe.matmul(PO[w % 2][:, (DH + 1) * (4 * q + g):(DH + 1) * (4 * q + g + 1)], E[:, s_ % 3, P * g:P * g + P],
                                   VG[:, w % 2, 4 * q + g, :], start=True, stop=True)
                mm.then_inc(pv_ready, 1)

            pe.wait_ge(t32_ready, 3 * NCH)
            pe.wait_ge(qk_low, NQ * NCH)
            for s_ in range(UNITS + LEAD + BEHIND):
                st = s_ - LEAD
                if st == -1:
                    v_groups(0)
                if s_ < UNITS:
                    maxima(s_)
                if 0 <= st < UNITS:
                    scores(st)
                if st >= BEHIND:
                    values(st - BEHIND)
                    if st % 4 == 2 and st // 4 + 1 < UNITS // 4:
                        v_groups(st // 4 + 1)

            def project(n):
                pe.wait_ge(split_done, 3 * n + 3)
                if n == NCH:
                    pe.wait_ge(weights, 4)
                for j in range(TPC):
                    t = TPC * (n - NCH) + j
                    if t >= 2:
                        pe.wait_ge(proj_mul, t - 1)
                    for p_, (a_, w_, r) in enumerate(PARTS):
                        mm = pe.matmul(QB[t % 2][:, 0:D], HT[0:r, n % 2, a_, P * j:P * j + P], WP[0:r, w_, :], start=(p_ == 0), stop=(p_ == 6))
                    mm.then_inc(proj_ready, 1)

            turn(NCH)
            for n in range(NCH, 2 * NCH):
                if n + 1 < 2 * NCH:
                    turn(n + 1)
                project(n)

            def fc1(n):
                pe.wait_ge(split_done, 3 * n + 3)
                if n == 2 * NCH:
                    pe.wait_ge(weights, 6)
                for m in range(NF):
                    idx = NF * (n - 2 * NCH) + m
                    if idx >= 3:
                        pe.wait_ge(gelu_sb, idx - 2)
                    for p_, (a_, w_, r) in enumerate(PARTS):
                        mm = pe.matmul(FB[idx % 3], W1[0:r, w_, P * m:P * m + P], HT[0:r, n % 2, a_, :], start=(p_ == 0), stop=(p_ == 6))
                    mm.then_inc(fc1_ready, 1)

            def fc2(n):
                c_ = n - 2 * NCH
                pe.wait_ge(g_low, NF * (c_ + 1))
                if c_ == 0:
                    pe.wait_ge(weights, 8)
                g = GT[c_ % 2]
                for j in range(TPC):
                    t = TPC * c_ + j
                    if t >= 2:
                        pe.wait_ge(y_mul, t - 1)
                    cols = slice(P * j, P * j + P)
                    for half in range(2):
                        pe.matmul(YB[t % 2][:, 0:D], FOUR[:, :], B2[:, half, :], start=(half == 0), stop=False)
                    for f in range(NF):
                        for a_, w_ in ((0, 0), (1, 0), (0, 1)):
                            mm = pe.matmul(YB[t % 2][:, 0:D], g[:, a_, f, cols], W2[:, w_, f, :], start=False, stop=(f == NF - 1 and w_ == 1))
                    mm.then_inc(fc2_ready, 1)

            turn(2 * NCH)
            for n in range(2 * NCH, 3 * NCH):
                if n + 1 < 3 * NCH:
                    turn(n + 1)
                fc1(n)
                if n > 2 * NCH:
                    fc2(n - 1)
            fc2(3 * NCH - 1)

        @block.scalar
        def _(act):
            act.wait_ge(in_c, 48)
            act.activation(SC[:, 0], CT[:, :, :], ACT.Exp, scale=-1.0).then_inc(silu_e, 1)

            def fill_out(n):
                act.wait_ge(fill_ready, n + 1)
                f = FILL[n % 2]
                if n == FPT:
                    cp = act.copy(PT2[:, :], f[:, 0:D])
                elif n < FX:
                    q, b = divmod(n - FW, 3)
                    k = BLK[b][1]
                    cp = act.copy(WT[0:k, b, 1 + 4 * WROWS * q:1 + 4 * WROWS * (q + 1)], f[0:k, 0:4 * WROWS])
                elif n < FZ:
                    i, b = divmod(n - FX, 3)
                    k = BLK[b][1]
                    cp = act.copy(XT[0:k, b, CH * i:CH * i + CH], f[0:k, :])
                elif n < FG:
                    i = n - FZ
                    cp = act.copy(ZT[:, CH * i:CH * i + CH], f[0:R, :])
                elif n < FM:
                    g, b = divmod(n - FG, 2)
                    cp = act.mul(GATE[:, g, b, :], f[:, 0:D], 1.0 / (FINE * FINE))
                else:
                    act.wait_ge(consts, 2)
                    fv = f[:, 0:24].rearrange("p (v m b) -> p v m b", v=4, b=B)
                    for v in range(4):
                        for m, rows in ((slice(0, 2), P), (slice(2, 3), 96)):
                            cp = act.activation(MOD[0:rows, v, m, :], fv[0:rows, v, m, :], ACT.Copy, scale=FINE,
                                                bias=FINE if v % 2 else 0.0)
                            if (v, rows) != (3, 96):
                                cp.then_inc(mod_part, 1)
                cp.then_inc(fill_done, 1)

            for k in range(R + LAG + 1):
                if k < R:
                    act.wait_ge(piv_inv, k + 1)
                    act.activation(RHO[:, k:k + 1], RI[:, k:k + 1], ACT.Sqrt, scale=4.0).then_inc(rho_ready, 1)
                    act.wait_ge(rho_ready, k + 1)
                    act.wait_ge(g_new, k + 2)
                    if k >= 4:
                        act.wait_ge(a_new, k - 2)
                    act.activation(ROWS[:, k % 4, k:R], PIV[k % 2][0:R, k:R], ACT.Copy, scale=RHO[:, k:k + 1]).then_inc(row_ready, 1)
                for n in fill_step.get(k - 1, ()):
                    fill_out(n)
                if k == SKEW_AT + R // 4:
                    act.wait_ge(skew_raw, 1)
                    sk = SKEW[0:R, 0:B * R].rearrange("p (i b) -> p b i", b=B)
                    for b in range(B):
                        act.copy(LT[:, b, :], sk[:, b, :]).then_inc(skew_sb, 1)
                if k == EXP_AT + 1:
                    act.wait_ge(skew_psum, 1)
                    for h in range(2):
                        act.mul(XX[:, R * h:R * h + R], EXPM[:, 0:R], (1 - 2 * h) * 2.0 ** -SQUARINGS).then_inc(skew_ready, 1)
                if EXP_AT + 1 < k <= EXP_AT + 1 + NEXP:
                    n = k - EXP_AT - 2
                    act.wait_ge(exp_psum, n + 1)
                    act.mul(YY[:, n % 2, :], EXPM[:, 0:2 * R], 1.0 / (4 - n) if n < 3 else 1.0).then_inc(exp_sb, 1)
            act.wait_ge(diag, 2)
            act.activation(dg[:, 2:3], dg[:, 0:1], ACT.Sqrt, scale=1.0).then_inc(root, 1)

            def norm_root(l):
                act.wait_ge(stats, l + 1)
                act.activation(ST[:, l, 1, :], ST[:, l, 0, :], ACT.Sqrt).then_inc(root2, 1)

            def turn_out(n, l):
                for b in range(3):
                    idx = 3 * n + b
                    act.wait_ge(tr_ready, idx + 1)
                    if idx >= 2:
                        act.wait_ge(split_done, idx - 1)
                    rows = 96 if b == 2 else P
                    batch = (n % NCH) // 2
                    src, dst = TRB[idx % 2][0:rows, :], T32[0:rows, idx % 2, :]
                    if l == 0:
                        src = src.rearrange("p (a m v) -> p a m v", a=TPC, m=8)
                        dst = dst.rearrange("p (m a v) -> p a m v", a=TPC, m=8)
                    if l is None:
                        cp = act.mul(dst, src, FINE)
                    else:
                        cp = act.activation(dst, src, ACT.Identity,
                                            scale=MOD[0:rows, 2 * l + 1, b, batch:batch + 1], bias=MOD[0:rows, 2 * l, b, batch:batch + 1])
                    cp.then_inc(t32_ready, 1)

            def qkv_out(n):
                for m, (f0, k) in enumerate(MT):
                    idx = NQ * n + m
                    act.wait_ge(qk_ready, idx + 1)
                    if idx >= 4:
                        act.wait_ge(qk_out[idx % 4], 16 * (idx // 4))
                    act.mul(QS[0:k, idx % 4, 0, :], QB[idx % 2][0:k, :], QSCALE / (FINE * FINE)).then_inc(qk_high, 1)

            norm_root(0)
            turn_out(0, 0)
            for n in range(NCH):
                if n + 1 < NCH:
                    turn_out(n + 1, 0)
                qkv_out(n)

            def exponentials(s_):
                act.wait_ge(s_ready, s_ + 1)
                if s_ >= 3:
                    act.wait_ge(pv_ready, s_ - 2)
                act.activation(E[:, s_ % 3, :], SB[s_ % 2], ACT.Exp, scale=DH ** -0.5 / (QSCALE * QSCALE)).then_inc(exp_done, 1)

            def v_out(w):
                act.wait_ge(vg_psum, w + 1)
                if w >= 2:
                    act.wait_ge(pv_ready, 4 * w - 4)
                act.mul(VG[:, w % 2, :, 0:DH], VB[:, 0:16 * DH].rearrange("p (g d) -> p g d", g=16), 1.0 / QSCALE).then_inc(vg_ready, 1)

            v_out(0)
            for st in range(UNITS):
                exponentials(st)
                if st >= BEHIND and st % 4 == 2 and st // 4 + 1 < UNITS // 4:
                    v_out(st // 4 + 1)

            turn_out(NCH, None)
            for n in range(NCH, 2 * NCH):
                if n + 1 < 2 * NCH:
                    turn_out(n + 1, None)
            norm_root(1)

            def gelu(n):
                for m in range(NF):
                    idx = NF * (n - 2 * NCH) + m
                    act.wait_ge(fc1_ready, idx + 1)
                    if idx >= 2:
                        act.wait_ge(g_low, idx - 1)
                    act.activation(G32[:, idx % 2, :], FB[idx % 3], ACT.Gelu, scale=1.0 / (FINE * FINE)).then_inc(gelu_sb, 1)

            turn_out(2 * NCH, 1)
            for n in range(2 * NCH, 3 * NCH):
                if n + 1 < 3 * NCH:
                    turn_out(n + 1, 1)
                gelu(n)

        @block.vector
        def _(dve):
            dve.wait_ge(gram, 1)
            dve.wait_ge(consts, 1)
            dve.tensor_copy(G[:, 0:R], MISC[0:R, 0:R]).then_inc(g_new, 1)
            dve.tensor_copy(A[:, :], PS[0:R, 0, :]).then_inc(a_new, 1)
            dve.wait_ge(g_new, 1)
            dve.wait_ge(a_new, 1)

            def silu_cond():
                dve.wait_ge(silu_e, 1)
                dve.tensor_scalar(SC[:, 1], SC[:, 0], 1.0, None, ALU.add).then_inc(silu_e, 1)
                dve.wait_ge(silu_e, 2)
                dve.reciprocal(SC[:, 2], SC[:, 1]).then_inc(silu_e, 1)
                dve.wait_ge(silu_e, 3)
                dve.tensor_tensor(SC[:, 3], SC[:, 2], CT[:, :, :], ALU.mult).then_inc(silu, 1)

            for k in range(R + LAG):
                g, j = k < R, k - LAG
                if g:
                    dve.wait_ge(piv_row, k + 1)
                    dve.reciprocal(RI[:, k:k + 1], PIV[k % 2][0:R, k:k + 1]).then_inc(piv_inv, 1)
                if j >= 0:
                    dve.wait_ge(a_row, j + 1)
                    dve.tensor_scalar(HALF[:, j:j + 1], AROW[0:R, j:j + 1], 0.0, 0.5, ALU.is_ge, ALU.subtract).then_inc(a_sign, 1)
                if g:
                    dve.wait_ge(piv_inv, k + 1)
                    dve.tensor_scalar(CG[:, k:k + 1], G[:, k:k + 1], RI[:, k:k + 1], below[:, k:k + 1], ALU.mult, ALU.mult).then_inc(gcoef, 1)
                if j >= 0:
                    dve.wait_ge(row_ready, j + 1)
                    dve.wait_ge(a_sign, j + 1)
                    dve.scalar_tensor_tensor(out=TR[:, j % 2, j:R], in0=ROWS[:, j % 4, j:R], scalar=HALF[:, j:j + 1],
                                             in1=AROW[0:R, j:R], op0=ALU.mult, op1=ALU.add).then_inc(a_sum, 1)
                if g:
                    dve.wait_ge(gcoef, k + 1)
                    dve.scalar_tensor_tensor(out=G[:, k + 1:R + k + 1], in0=PIV[k % 2][0:R, k + 1:R + k + 1], scalar=CG[:, k:k + 1],
                                             in1=G[:, k + 1:R + k + 1], op0=ALU.mult, op1=ALU.add).then_inc(g_new, 1)
                if j >= 0:
                    dve.wait_ge(a_sum, j + 1)
                    dve.reciprocal(RA[:, j:j + 1], TR[:, j % 2, j:j + 1]).then_inc(a_piv, 1)
                    dve.wait_ge(a_piv, j + 1)
                    dve.tensor_scalar(CA[:, j:j + 1], A[:, j:j + 1], RA[:, j:j + 1], below[:, j:j + 1], ALU.mult, ALU.mult).then_inc(acoef, 1)
                    dve.wait_ge(acoef, j + 1)
                    lo = min(j + 1, R - 1)
                    dve.scalar_tensor_tensor(out=A[:, lo:R], in0=TR[:, j % 2, lo:R], scalar=CA[:, j:j + 1],
                                             in1=A[:, lo:R], op0=ALU.mult, op1=ALU.add).then_inc(a_new, 1)
                if k == 2:
                    silu_cond()
            dve.wait_ge(a_new, R + 1)
            for n, src in ((0, RI), (1, HALF)):
                dve.tensor_tensor_reduce(TR[:, n, :], src[:, :], ident[0:R, 0:R], 1.0, 0.0, ALU.mult, ALU.add, dg[:, n:n + 1]).then_inc(diag, 1)
            dve.wait_ge(root, 1)
            dve.wait_ge(diag, 2)
            dve.reciprocal(dg[:, 3:4], dg[:, 2:3]).then_inc(root, 1)
            dve.wait_ge(root, 2)
            dve.tensor_scalar(dg[:, 4:5], dg[:, 3:4], dg[:, 0:1], dg[:, 2:3], ALU.mult, ALU.add).then_inc(root, 1)
            dve.wait_ge(root, 3)
            dve.wait_ge(g_new, R + 1)
            for g in range(2):
                dve.tensor_scalar(V2[R * g:R * g + R, :], G[:, R:2 * R], dg[:, 4:5], dg[:, 1:2], ALU.mult, ALU.mult).then_inc(basis, 1)
            dve.wait_ge(rot_psum, 1)
            dve.tensor_copy(T1[:, :], EXPM[:, 0:R]).then_inc(rot_sb, 1)
            dve.wait_ge(rot_psum, 2)
            dve.tensor_copy(NTs[:, :], SKEW[:, 0:R]).then_inc(rot_sb, 1)
            dve.wait_ge(rot_psum, 3)
            for b in range(B):
                dve.tensor_copy(ROT[:, b, :], PIV[b][0:R, 0:D]).then_inc(rot_sb, 1)
            def stat(l, t):
                idx = NT * l + t
                if t >= 2 or l:
                    dve.wait_ge(bn_s, 2 * idx - 2)
                dve.bn_stats(BN[:, t % 2, :], X[:, t, :]).then_inc(bn_s, 1)
                dve.wait_ge(bn_s, 2 * idx + 1)
                dve.bn_aggr(MV[:, l, t, :], BN[:, t % 2, :]).then_inc(bn_s, 1)

            def norm_scales(l):
                s_ = ST[:, l]
                n0 = 5 * l
                dve.wait_ge(bn_s, 2 * NT * (l + 1))
                dve.tensor_scalar(s_[:, 0, :], MV[:, l, :, 1], EPS, None, ALU.add).then_inc(stats, 1)
                dve.wait_ge(root2, l + 1)
                dve.wait_ge(stats, l + 1)
                dve.reciprocal(s_[:, 2, :], s_[:, 1, :]).then_inc(scales, 1)
                dve.wait_ge(scales, n0 + 1)
                dve.tensor_tensor(s_[:, 3, :], s_[:, 2, :], s_[:, 2, :], ALU.mult).then_inc(scales, 1)
                dve.wait_ge(scales, n0 + 2)
                dve.tensor_tensor(s_[:, 4, :], s_[:, 3, :], s_[:, 0, :], ALU.mult).then_inc(scales, 1)
                dve.wait_ge(scales, n0 + 3)
                dve.tensor_scalar(s_[:, 5, :], s_[:, 4, :], -0.5, 1.5, ALU.mult, ALU.add).then_inc(scales, 1)
                dve.wait_ge(scales, n0 + 4)
                dve.tensor_tensor(s_[:, 6, :], s_[:, 5, :], s_[:, 2, :], ALU.mult).then_inc(scales, 1)
                dve.wait_ge(scales, n0 + 5)

            def source(n, l):
                if n >= 2:
                    dve.wait_ge(tr_ready, 3 * n - 3)
                for j in range(TPC):
                    t = TPC * (n % NCH) + j
                    if l is None:
                        dve.tensor_copy(XN[:, n % 2, j, 0:D], stage[:, D * t:D * t + D]).then_inc(xn_main, 1)
                    else:
                        dve.tensor_scalar(XN[:, n % 2, j, 0:D], X[:, t, :], MV[:, l, t, 0:1], ST[:, l, 6, t:t + 1],
                                          ALU.subtract, ALU.mult).then_inc(xn_main, 1)
                dve.wait_ge(xn_main, TPC * (n + 1))
                dve.tensor_copy(XN[:, n % 2, :, D:DX].rearrange("p t (a c) -> p t a c", a=2),
                                XN[:, n % 2, :, D - 32:D].unsqueeze(2).broadcast_to([P, TPC, 2, 32])).then_inc(xn_ready, 1)

            def split(n):
                for b in range(3):
                    idx = 3 * n + b
                    dve.wait_ge(t32_ready, idx + 1)
                    if b == 0 and n >= 2:
                        if n < NCH:
                            dve.wait_ge(qk_ready, NQ * (n - 1))
                        elif NCH + 2 <= n < 2 * NCH:
                            dve.wait_ge(proj_ready, TPC * (n - NCH - 1))
                        elif n >= 2 * NCH + 2:
                            dve.wait_ge(fc1_ready, NF * (n - 2 * NCH - 1))
                        elif n >= 2 * NCH:
                            dve.wait_ge(proj_ready, TPC * (n - NCH - 1))
                    rows = slice(0, 96) if b == 2 else slice(0, P)
                    high = HT[rows, n % 2, 4 if b == 2 else b, :]
                    dve.tensor_copy(high, T32[rows, idx % 2, :]).then_inc(cast_done, 1)
                    dve.wait_ge(cast_done, idx + 1)
                    rows = slice(32, 64) if b == 2 else slice(0, P)
                    low = HT[rows, n % 2, 4 if b == 2 else 2 + b, :]
                    high = HT[rows, n % 2, 4 if b == 2 else b, :]
                    dve.tensor_tensor(low, T32[rows, idx % 2, :], high, ALU.subtract).then_inc(split_done, 1)

            def ones_rows(n):
                for a_ in range(2):
                    dve.memset(HT[96:P, a_, 4, :], FINE).then_inc(ht_ones, 1)
                dve.wait_ge(ht_ones, 2 * n + 2)

            for t in range(NT):
                dve.wait_ge(delta_ready, t + 1)
                dve.tensor_tensor(X[:, t, :], FILL[t % 2][:, 0:D], X[:, t, :], ALU.add).then_inc(x_rot, 1)
                if t >= 1:
                    dve.wait_ge(x_rot, t)
                    stat(0, t - 1)
            dve.wait_ge(x_rot, NT)
            stat(0, NT - 1)
            norm_scales(0)
            dve.wait_ge(fill_done, NFILL)
            ones_rows(0)
            source(0, 0)
            source(1, 0)
            split(0)
            for n in range(NCH):
                if n + 1 < NCH:
                    split(n + 1)
                for m, (f0, k) in enumerate(MT):
                    idx = NQ * n + m
                    dve.wait_ge(qk_high, idx + 1)
                    dve.scalar_tensor_tensor(out=QS[0:k, idx % 4, 1, :], in0=QB[idx % 2][0:k, :], scalar=QSCALE / (FINE * FINE),
                                             in1=QS[0:k, idx % 4, 0, :], op0=ALU.mult, op1=ALU.subtract).then_inc(qk_low, 1)
                if n + 2 < NCH:
                    source(n + 2, 0)

            def maximum(s_):
                n, u = divmod(s_, 16)
                dve.wait_ge(mx_ready, s_ + 1)
                dve.tensor_reduce(MX[:, n, 4 * u:4 * u + 4], MXB[s_ % 2].rearrange("p (g c) -> p g c", g=4), AX.X, ALU.max,
                                  negate=True).then_inc(mx_used, 1)
                if u == 15:
                    dve.wait_ge(mx_used, s_ + 1)
                    dve.tensor_scalar(MR[:, n, :], MX[:, n, :], 1.0 / MROW, None, ALU.mult).then_inc(mx_half, 1)

            def normalise(w):
                n, q = divmod(w, 4)
                dve.wait_ge(pv_ready, 4 * w + 4)
                if w == 0:
                    dve.wait_ge(weights, 8)
                if w >= 2:
                    dve.wait_ge(o_norm, w - 1)
                po = PO[w % 2][:, 0:16 * (DH + 1)].rearrange("p (g d) -> p g d", g=16)
                dve.reciprocal(RD[:, w % 2, :], po[:, :, DH]).then_inc(o_sum, 1)
                dve.wait_ge(o_sum, w + 1)
                dve.tensor_tensor(AO[:, n // 2, :, :, 4 * (n % 2) + q, :],
                                  po[:, :, 0:DH].rearrange("p (a e) d -> p a e d", e=2),
                                  RD[:, w % 2, :].rearrange("p (a e) -> p a e", e=2).unsqueeze(3).broadcast_to([P, 8, 2, DH]),
                                  ALU.mult).then_inc(o_norm, 1)

            for s_ in range(UNITS + LEAD + BEHIND):
                if s_ < UNITS:
                    maximum(s_)
                k = s_ - LEAD - BEHIND - 3
                if k >= 0 and k % 4 == 0:
                    normalise(k // 4)
            dve.wait_ge(o_norm, UNITS // 4)
            source(NCH, None)
            source(NCH + 1, None)
            split(NCH)
            for n in range(NCH, 2 * NCH):
                if n + 1 < 2 * NCH:
                    split(n + 1)
                for j in range(TPC):
                    t = TPC * (n - NCH) + j
                    dve.wait_ge(proj_ready, t + 1)
                    if t >= 6:
                        dve.wait_ge(x_mid, t - 5)
                    dve.tensor_tensor(YT[:, t % 6, :], QB[t % 2][:, 0:D], GATE[:, 0, t // 8, :], ALU.mult).then_inc(proj_mul, 1)
                    dve.wait_ge(proj_mul, t + 1)
                    dve.tensor_tensor(X[:, t, :], X[:, t, :], YT[:, t % 6, :], ALU.add).then_inc(x_mid, 1)
                    dve.wait_ge(x_mid, t + 1)
                    stat(1, t)
                if n + 2 < 2 * NCH:
                    source(n + 2, None)
            norm_scales(1)
            source(2 * NCH, 1)
            source(2 * NCH + 1, 1)
            split(2 * NCH)

            def gelu_split(n):
                c_ = n - 2 * NCH
                for m in range(NF):
                    idx = NF * c_ + m
                    dve.wait_ge(gelu_sb, idx + 1)
                    if m == 0 and c_ >= 2:
                        dve.wait_ge(fc2_ready, TPC * (c_ - 1))
                    dve.tensor_scalar(GT[c_ % 2][:, 0, m, :], G32[:, idx % 2, :], FINE, None, ALU.mult).then_inc(g_high, 1)
                    dve.wait_ge(g_high, idx + 1)
                    dve.scalar_tensor_tensor(out=GT[c_ % 2][:, 1, m, :], in0=G32[:, idx % 2, :], scalar=FINE,
                                             in1=GT[c_ % 2][:, 0, m, :], op0=ALU.mult, op1=ALU.subtract).then_inc(g_low, 1)

            def result(n):
                for j in range(TPC):
                    t = TPC * (n - 2 * NCH) + j
                    dve.wait_ge(fc2_ready, t + 1)
                    if t >= 6:
                        dve.wait_ge(y_out[t % 6], 16 * (t // 6))
                    dve.tensor_tensor(YT[:, t % 6, :], YB[t % 2][:, 0:D], GATE[:, 1, t // 8, :], ALU.mult).then_inc(y_mul, 1)
                    dve.wait_ge(y_mul, t + 1)
                    dve.tensor_tensor(YT[:, t % 6, :], YT[:, t % 6, :], X[:, t, :], ALU.add).then_inc(y_ready, 1)

            for n in range(2 * NCH, 3 * NCH):
                if n + 1 < 3 * NCH:
                    split(n + 1)
                gelu_split(n)
                if n + 2 < 3 * NCH:
                    source(n + 2, 1)
                if n > 2 * NCH:
                    result(n - 1)
            result(3 * NCH - 1)


_INS = ["x", "cond_1152", "L0_cond_P", "L0_cond_W", "L0_cond_b", "L1_cond_qkv_w", "L1_cond_qkv_b", "L1_cond_proj_w",
        "L1_cond_proj_b", "L1_cond_fc1_w", "L1_cond_fc1_b", "L1_cond_fc2_w", "L1_cond_fc2_b", "L1_cond_ada_w", "L1_cond_ada_b"]


def kernel(**inputs):
    import numpy as _np
    import concourse.bacc as _bacc
    from concourse import mybir as _mybir
    from concourse.bass_utils import run_bass_kernel_spmd as _run

    nc = _bacc.Bacc("TRN2", target_bir_lowering=False, num_devices=1)
    arrays, args = {}, []
    for name in _INS:
        a = _np.ascontiguousarray(inputs[name])
        arrays[f"in_{name}_dram"] = a
        args.append(nc.dram_tensor(f"in_{name}_dram", a.shape, _mybir.dt.from_np(a.dtype), kind="ExternalInput").ap())
    args.append(nc.dram_tensor("out_0_dram", (2, 1024, 288), _mybir.dt.float32, kind="ExternalOutput").ap())
    build(nc, *args)
    r = _run(nc, [arrays], core_ids=[0])
    return r.results[0]["out_0_dram"]
```

```python
from contextlib import ExitStack

import concourse.bass as bass
from concourse import mybir

F32 = mybir.dt.float32
F16 = mybir.dt.float16
ALU = mybir.AluOpType
ACT = mybir.ActivationFunctionType
AX = mybir.AxisListType

B, T, D = 2, 1024, 288
R = 64
H, DH = 16, 18
MLP = 4 * D
P = 128
NT = B * T // P
CH = 512
NCH = B * T // CH
TPC = CH // P
BLK = ((0, 128), (128, 128), (256, 32))
NF = MLP // P
NSKEW = R * (R - 1) // 2
WTILES = 16
WROWS = NSKEW // WTILES
SQUARINGS = 16
FINE = 64.0
EPS = 1e-6


def build(nc, x, c, pmat, wskew, bskew, qkv_w, qkv_b, proj_w, proj_b, fc1_w, fc1_b, fc2_w, fc2_b, ada_w, ada_b, out):
    with ExitStack() as ctx:
        def sb(name, shape, dt=F32):
            return ctx.enter_context(nc.sbuf_tensor(name, shape, dt))

        def sem(name):
            return ctx.enter_context(nc.semaphore(name))

        psum = ctx.enter_context(nc.psum_tensor("psum", [P, 8, 512], F32))
        bank = [psum[:, i, :] for i in range(8)]

        X = sb("X", [P, NT, D])
        big = sb("big", [P, 22528])
        WL = big[0:WROWS, 0:WTILES * D].rearrange("p (t n) -> p t n", t=WTILES)
        o = WTILES * D
        ADA = big[:, o:o + 18 * D].rearrange("p (b n) -> p b n", b=3)
        o += 18 * D
        SWP = big[:, o:o + 3 * D].rearrange("p (b n) -> p b n", b=3)
        o += 3 * D
        SW1 = big[:, o:o + 12 * D].rearrange("p (b n) -> p b n", b=3)
        o += 12 * D
        SCB = big[0:WROWS, o:o + 6 * D].rearrange("p (s b n) -> p s b n", s=3, b=B)
        o += 6 * D
        SB2 = big[0:1, o:o + D]
        assert o + D <= 22528 - 3 * B * T
        XT = big[:, 22528 - 3 * B * T:22528].rearrange("p (b t) -> p b t", b=3)
        stage = sb("stage", [P, 18 * D])
        SWQ = stage[:, 0:9 * D].rearrange("p (b n) -> p b n", b=3)
        SW2 = stage[:, 9 * D:18 * D].rearrange("p (b n) -> p b n", b=NF)
        CB = stage[0:WROWS, 9 * D:11 * D].rearrange("p (b n) -> p b n", b=B)
        JUNK = stage[0:WROWS, 11 * D:15 * D].rearrange("p (a n) -> p a n", a=4)
        WQ = sb("WQ", [P, 5, 3 * D], F16)
        WP = sb("WP", [P, 5, D], F16)
        W1 = sb("W1", [P, 5, MLP], F16)
        W2 = sb("W2", [P, 2, NF, D], F16)
        B2 = sb("B2", [1, 2, D], F16)
        GATE = sb("GATE", [P, 2, B, D])
        MOD = sb("MOD", [P, 4, 3, B])
        ident = sb("ident", [P, P])
        ones = sb("ones", [P, P])

        scratch = sb("scratch", [P, 9320])
        used = [0]

        def part(rows, *dims):
            n = 1
            for d in dims:
                n *= d
            a = scratch[0:rows, used[0]:used[0] + n]
            used[0] += n
            if len(dims) == 2:
                a = a.rearrange("p (a b) -> p a b", a=dims[0])
            if len(dims) == 3:
                a = a.rearrange("p (a b c) -> p a b c", a=dims[0], b=dims[1])
            return a

        ZT = part(P, T)
        VR = part(WROWS, 2, B, WTILES)
        BR = part(WROWS, WTILES)
        ADAB = part(1, 6 * D)
        ROT = part(P, D)
        AD = part(P, 2, D)
        SC32 = part(P, 3, 32)
        below = part(R, R)
        lowrow = sb("lowrow", [P, 1])
        TWO = part(P, P)
        II = part(P, P)
        PS = part(P, 3, R)
        PT2 = part(P, D)
        CT = part(P, 3, B)
        SC = part(P, 3, 3, B)
        G = part(R, 2 * R)
        A = part(R, R)
        RI = part(R, R)
        SG = part(R, R)
        RHO = part(R, R)
        ROWS = part(R, 4, R)
        CG = part(R, R)
        CA = part(R, R)
        RA = part(R, R)
        DJ = part(R, 2, R)
        dg = part(R, 8)
        V2 = part(P, R)
        UP = part(R, B, R)
        NEGI = part(R, R)
        XX = part(P, 2 * R)
        YY = part(P, 2, 2 * R)
        T1 = part(P, R)
        NTs = part(P, R)

        ST = sb("ST", [P, 2, 8, NT])
        MV = sb("MV", [P, 2, NT, 2])
        BN = sb("BN", [P, 2, 6])
        FOUR = sb("FOUR", [1, P], F16)
        SELV = sb("SELV", [P, DH], F16)
        MX = sb("MX", [P, NCH, 64])
        MR = sb("MR", [P, NCH, 64], F16)
        RD = sb("RD", [P, 2, 16])
        VG = sb("VG", [P, 2, 16, DH + 1])
        o = 0
        DX = D + 64
        XN = scratch[:, o:o + 2 * TPC * DX].rearrange("p (a t n) -> p a t n", a=2, t=TPC)
        o += 2 * TPC * DX
        T32 = scratch[:, o:o + 2 * CH].rearrange("p (a n) -> p a n", a=2)
        o += 2 * CH
        HT = scratch[:, o:o + 5 * CH].bitcast(F16).rearrange("p (a s n) -> p a s n", a=2, s=5)
        o += 5 * CH
        QS = scratch[:, o:o + 4 * CH].bitcast(F16).rearrange("p (a s n) -> p a s n", a=4, s=2)
        assert o + 4 * CH <= 9320
        QKT = [big[:, 14336:22528].bitcast(F16).rearrange("p (w c) -> p w c", w=2),
               big[:, 0:8192].bitcast(F16).rearrange("p (w c) -> p w c", w=2)]
        VT = big[:, 8192:12288].bitcast(F16)
        E = big[:, 12288:12288 + 3 * CH].rearrange("p (a n) -> p a n", a=3)
        CST = big[:, 12288 + 3 * CH:14336].bitcast(F16)
        MASKQ, MASKK = CST[0:8, 0:CH], CST[0:9, CH:2 * CH]
        AO = stage[:, 0:NT * D].rearrange("p (b a e c d) -> p b a e c d", b=B, a=8, e=2, c=8)
        GT = [big[:, 0:NF * CH].bitcast(F16).rearrange("p (s f n) -> p s f n", s=2, f=NF),
              big[:, NF * CH:2 * NF * CH].bitcast(F16).rearrange("p (s f n) -> p s f n", s=2, f=NF)]
        G32 = big[:, 2 * NF * CH:2 * NF * CH + 2 * CH].rearrange("p (a n) -> p a n", a=2)
        YT = big[:, 2 * (NF + 1) * CH:2 * (NF + 1) * CH + 6 * D].rearrange("p (a n) -> p a n", a=6)
        vd = nc.dram_tensor("skew_entries", [B, NSKEW], F32, kind="Internal").ap()
        qkd = nc.dram_tensor("qkv_halves", [2, NCH, 3 * D, CH], F16, kind="Internal").ap()

        in_p, in_c, in_cb, in_w, in_br, in_ada, in_adab = (sem(n) for n in ("in_p", "in_c", "in_cb", "in_w", "in_br", "in_ada", "in_adab"))
        in_wq, in_wp, in_w1, in_w2 = (sem(n) for n in ("in_wq", "in_wp", "in_w1", "in_w2"))
        in_x = [sem(f"in_x{i}") for i in range(NCH)]
        consts = sem("consts")
        pool_step = sem("pool_step")
        ct_clear = sem("ct_clear")
        silu_e = sem("silu_e")
        silu = sem("silu")
        cb_e, cb_done = sem("cb_e"), sem("cb_done")
        v_sum, v_all, v_out_done, up_clear, up_in = sem("v_sum"), sem("v_all"), sem("v_out_done"), sem("up_clear"), sem("up_in")
        gram = sem("gram")
        state0 = sem("state0")
        piv_row, piv_inv, gcoef, g_new = sem("piv_row"), sem("piv_inv"), sem("gcoef"), sem("g_new")
        rho_ready, row_ready = sem("rho_ready"), sem("row_ready")
        a_row, a_piv, acoef, a_new, a_sign = sem("a_row"), sem("a_piv"), sem("acoef"), sem("a_new"), sem("a_sign")
        fill_ready, fill_done = sem("fill_ready"), sem("fill_done")
        skew_psum, skew_ready = sem("skew_psum"), sem("skew_ready")
        exp_psum, exp_sb = sem("exp_psum"), sem("exp_sb")
        diag, root, basis = sem("diag"), sem("root"), sem("basis")
        rot_psum, rot_sb = sem("rot_psum"), sem("rot_sb")
        delta_ready, x_rot = sem("delta_ready"), sem("x_rot")
        weights = sem("weights")
        mod_part = sem("mod_part")
        bn_s, stats, root2, scales = sem("bn_s"), sem("stats"), sem("root2"), sem("scales")
        ht_ones = sem("ht_ones")
        xn_ready, tr_ready, t32_ready, cast_done, split_done = (
            sem(n) for n in ("xn_ready", "tr_ready", "t32_ready", "cast_done", "split_done"))
        qk_ready, qk_high, qk_low = sem("qk_ready"), sem("qk_high"), sem("qk_low")
        qk_out = [sem(f"qk_out{i}") for i in range(4)]
        att_const = sem("att_const")
        att_rows = [sem(f"att_rows{i}") for i in range(2)]
        qk_in = [sem(f"qk_in{i}") for i in range(NCH)]
        v_in = [sem(f"v_in{i}") for i in range(NCH)]
        max_in = [sem(f"max_in{i}") for i in range(NCH)]
        mx_ready, mx_used, mx_half = sem("mx_ready"), sem("mx_used"), sem("mx_half")
        s_ready, exp_done = sem("s_ready"), sem("exp_done")
        vg_psum, vg_ready, pv_ready, o_sum, o_norm = (sem(n) for n in ("vg_psum", "vg_ready", "pv_ready", "o_sum", "o_norm"))
        proj_ready, proj_mul, x_mid = sem("proj_ready"), sem("proj_mul"), sem("x_mid")
        fc1_ready, gelu_sb, g_high, g_low = sem("fc1_ready"), sem("gelu_sb"), sem("g_high"), sem("g_low")
        fc2_ready, y_mul, y_ready = sem("fc2_ready"), sem("y_mul"), sem("y_ready")
        y_out = [sem(f"y_out{i}") for i in range(6)]
        xn_main = sem("xn_main")

        PIV = [bank[0], bank[1]]
        AROW = [bank[2], bank[5]]
        FILL = [bank[3], bank[4]]
        EXPM = bank[6]
        MISC = bank[7]

        work = ["P'", (0, 0), (0, 1), (0, 2), (2, 0), (2, 1), (2, 2), (1, 0), (0, 3), (1, 1), (1, 2), (3, 0), (3, 1), (3, 2),
                "ada 0", "ada 1", (1, 3), "mod"]
        ADA_ROWS = ((0, 1, 3, 4), (2, 5))
        FG = len(work)
        NFILL = FG + 4
        XDONE = [work.index((i + 2, 2)) + 1 for i in range(2)]
        pieces = []
        for n, w in enumerate(work):
            pieces += [(n, p_) for p_ in range({"P'": 2, "mod": 1}.get(w, 4 if w[0] == "a" else 6 if w[1] == 3 else 4))]
        last_piece = {n: i for i, (n, _) in enumerate(pieces)}
        FIRST = 5
        PER = 2
        V_AT = 4
        V_PER = 2
        EXP_AT = 43
        NEXP = 3 + SQUARINGS
        LAG = 2
        assert FIRST + len(pieces) // PER < R + LAG and EXP_AT + NEXP + 2 < R + LAG

        TRB = [bank[0], bank[1]]
        QB = [bank[2], bank[3]]
        MXB, SB, VB, PO = [bank[0], bank[1]], [bank[2], bank[3]], bank[4], [bank[5], bank[6]]
        FB = [bank[2], bank[3], bank[4]]
        YB = [bank[5], bank[6]]
        PARTS = ((0, 0, P), (1, 1, P), (2, 0, P), (3, 1, P), (0, 2, P), (1, 3, P), (4, 4, 98))
        MT = [(126 * m, min(126, 3 * D - 126 * m)) for m in range(7)]
        NQ = len(MT)
        UNITS = 16 * NCH
        QSCALE = 8.0
        MROW = 16.0
        MASK = (240.0, -60000.0)
        HALVES = 3 * DH
        MROWS = HALVES + 8
        LEAD = 22
        BEHIND = 2

        def operand(n, w, u, g, rows):
            r = R * (n % 2)
            return QKT[n // 2][r:r + rows, w, 4 * u + g:4 * u + g + 64 * P - 63:64]

        block = ctx.enter_context(nc.Block())

        @block.sync
        def _(sp):
            for b, (r0, n) in enumerate(BLK):
                sp.dma_start(PS[0:n, b, :], pmat[r0:r0 + n, :]).then_inc(in_p, 16)
            sp.wait_ge(ct_clear, 1)
            for b, (r0, n) in enumerate(BLK):
                sp.dma_start(CT[0:n, b, :], c[:, r0:r0 + n].rearrange("b p -> p b"), allow_slow_non_contiguous=True).then_inc(in_c, 16)
            sp.dma_start(CB, c.unsqueeze(0).broadcast_to([WROWS, B, D])).then_inc(in_cb, 16)
            sp.dma_start(WL, wskew.rearrange("(p t) n -> p t n", p=WROWS)).then_inc(in_w, 16)
            for i in (0, 2, 1, 3):
                b, a = divmod(TPC * i, 8)
                sp.dma_start(X[:, TPC * i:TPC * i + TPC, :], x[b].rearrange("(p a) d -> p a d", a=8)[:, a:a + TPC, :]).then_inc(in_x[i], 16)
            sp.dma_start(BR, bskew.rearrange("(p t) -> p t", p=WROWS)).then_inc(in_br, 16)

            def staged(w, bias, dst, s_):
                sp.dma_start(dst[:, 0:2, :], w[0:2 * P, :].rearrange("(b p) n -> p b n", p=P)).then_inc(s_, 16)
                for g in range(3):
                    sp.dma_start(dst[32 * g:32 * g + 32, 2, :], w[2 * P:D, :]).then_inc(s_, 16)
                for g in range(2):
                    sp.dma_start(dst[96 + g:97 + g, 2, :], bias.rearrange("(a n) -> a n", a=1)).then_inc(s_, 16)

            staged(qkv_w, qkv_b, SWQ, in_wq)
            sp.dma_start(ADAB[:, :], ada_b.rearrange("(a n) -> a n", a=1)).then_inc(in_adab, 16)
            for b, (r0, n) in enumerate(BLK):
                sp.dma_start(ADA[0:n, b, :], ada_w[r0:r0 + n, :]).then_inc(in_ada, 16)
            sp.wait_ge(v_all, 1)
            sp.dma_start(vd.rearrange("b (p t) -> p b t", p=WROWS), VR[:, 1]).then_inc(v_out_done, 16)
            sp.wait_ge(v_out_done, 16)
            sp.wait_ge(up_clear, 1)
            for i in range(R - 1):
                at = i * (2 * R - 1 - i) // 2
                sp.dma_start(UP[i:i + 1, :, i + 1:R], vd[:, at:at + R - 1 - i].unsqueeze(0),
                             allow_slow_non_contiguous=True).then_inc(up_in, 16)
            sp.dma_start(SW2, fc2_w.rearrange("(b p) n -> p b n", p=P)).then_inc(in_w2, 16)
            sp.dma_start(SB2[:, :], fc2_b.rearrange("(a n) -> a n", a=1)).then_inc(in_w2, 16)
            staged(proj_w, proj_b, SWP, in_wp)
            staged(fc1_w, fc1_b, SW1, in_w1)
            def halves_out(n):
                for m, (f0, k) in enumerate(MT):
                    idx = NQ * n + m
                    sp.wait_ge(qk_low, idx + 1)
                    sp.dma_start(qkd[:, n, f0:f0 + k, :].rearrange("c f n -> f c n"), QS[0:k, idx % 4, :, :]).then_inc(qk_out[idx % 4], 16)
                for j in range(4):
                    sp.wait_ge(qk_out[j], 16 * len(range(j, NQ * (n + 1), 4)))

            def rows_in(dst, r, n, half, w, s_):
                sp.dma_start(dst[r:r + DH, :].rearrange("p (h c) -> p h c", h=H),
                             qkd[half, n, D * w:D * w + D, :].rearrange("(h d) c -> d h c", h=H)).then_inc(s_, 16)

            def qk_rows(n):
                for w, halves in ((0, (0, 1, 0)), (1, (0, 0, 1))):
                    for c_, half in enumerate(halves):
                        rows_in(QKT[n // 2][:, w, :], R * (n % 2) + DH * c_, n, half, w, qk_in[n])

            def v_rows(n):
                for half in range(2):
                    rows_in(VT, R * (n % 2) + DH * half, n, half, 2, v_in[n])

            def const_rows(n):
                r = R * (n % 2) + HALVES
                for w, k, src in ((0, 8, MASKQ), (1, 9, MASKK)):
                    sp.dma_start(QKT[n // 2][r:r + k, w, :].rearrange("p (h c) -> p h c", h=H),
                                 src.unsqueeze(1).broadcast_to([k, H, CH])).then_inc(att_rows[n // 2], 16)

            def max_row(n):
                sp.wait_ge(mx_half, n + 1)
                r = R * (n % 2) + MROWS
                sp.dma_start(QKT[n // 2][r:r + 1, 0, :].rearrange("p (j u) -> p j u", j=P), MR[:, n, :]).then_inc(max_in[n], 16)

            sp.wait_ge(att_const, 1)
            sp.wait_ge(fill_done, NFILL)
            const_rows(0)
            const_rows(1)
            halves_out(0)
            qk_rows(0)
            sp.wait_ge(weights, 8)
            v_rows(0)
            halves_out(1)
            qk_rows(1)
            v_rows(1)
            const_rows(2)
            const_rows(3)
            halves_out(2)
            qk_rows(2)
            halves_out(3)
            qk_rows(3)
            max_row(0)
            sp.wait_ge(vg_psum, 4)
            v_rows(2)
            max_row(1)
            sp.wait_ge(vg_psum, 8)
            v_rows(3)
            max_row(2)
            max_row(3)

            for t in range(NT):
                sp.wait_ge(y_ready, t + 1)
                sp.dma_start(out[t // 8].rearrange("(p a) d -> p a d", a=8)[:, t % 8, :], YT[:, t % 6, :]).then_inc(y_out[t % 6], 16)
            for j in range(6):
                sp.wait_ge(y_out[j], 16 * len(range(j, NT, 6)))

        @block.gpsimd
        def _(pool):
            steps = [0]

            def chain(ins):
                steps[0] += 1
                ins.then_inc(pool_step, 1)
                pool.wait_ge(pool_step, steps[0])

            pool.memset(CT[:, :, :], 0.0).then_inc(ct_clear, 1)
            chain(pool.memset(ident[:, :], 0.0))
            chain(pool.memset(below[:, :], -1.0))
            chain(pool.affine_select(out=ident[:, :], in_=ident[:, :], compare_op=ALU.not_equal, fill=1.0, base=0,
                                     pattern=[[-1, P]], channel_multiplier=1))
            chain(pool.affine_select(out=below[:, :], in_=below[:, :], compare_op=ALU.is_gt, fill=0.0, base=0,
                                     pattern=[[-1, R]], channel_multiplier=1))
            chain(pool.memset(SC32[:, :, :], 0.0))
            chain(pool.memset(ones[:, :], 1.0))
            pool.tensor_copy(G[:, R:2 * R], ident[0:R, 0:R]).then_inc(consts, 1)
            pool.wait_ge(consts, 1)
            chain(pool.tensor_scalar(TWO[:, :], ident[:, :], 2.0, None, ALU.mult))
            chain(pool.tensor_scalar(NEGI[:, :], ident[0:R, 0:R], -1.0, None, ALU.mult))
            pool.memset(UP[:, :, :], 0.0).then_inc(up_clear, 1)
            for g in range(2):
                for h in range(2):
                    chain(pool.tensor_copy(II[R * g:R * g + R, R * h:R * h + R], ident[R * g:R * g + R, R * g:R * g + R]))
            pool.memset(MOD[:, :, :, :], 0.0).then_inc(consts, 1)
            pool.wait_ge(consts, 2)
            chain(pool.memset(lowrow[:, :], 0.0))
            chain(pool.memset(lowrow[64:P, :], -1.0))
            chain(pool.affine_select(out=lowrow[96:P, :], in_=lowrow[96:P, :], compare_op=ALU.not_equal, fill=0.0, base=0,
                                     pattern=[[0, 1]], channel_multiplier=1))
            chain(pool.tensor_copy(SELV[:, :], ident[:, 0:DH]))
            for j in (DH, R, R + DH):
                chain(pool.tensor_tensor(SELV[:, :], SELV[:, :], ident[:, j:j + DH], ALU.add))
            chain(pool.memset(VG[:, :, :, DH:DH + 1], 1.0))
            chain(pool.memset(FOUR[:, :], FINE))
            for src, dst, n, s_ in ((SWQ, WQ, 3 * D, in_wq), (SWP, WP, D, in_wp), (SW1, W1, MLP, in_w1)):
                pool.wait_ge(s_, 96)
                chain(pool.tensor_scalar(src[:, 0:2, :], src[:, 0:2, :], FINE, None, ALU.mult))
                chain(pool.tensor_copy(dst[:, 0:2, :], src[:, 0:2, :]))
                pool.tensor_tensor(dst[:, 2:4, :], src[:, 0:2, :], dst[:, 0:2, :], ALU.subtract).then_inc(weights, 1)
                r = slice(0, 98)
                chain(pool.tensor_scalar(src[r, 2, :], src[r, 2, :], FINE, None, ALU.mult))
                chain(pool.tensor_copy(dst[r, 4, :], src[r, 2, :]))
                chain(pool.tensor_scalar(dst[r, 4, :], dst[r, 4, :], lowrow[r, :], None, ALU.mult))
                pool.tensor_tensor(dst[r, 4, :], src[r, 2, :], dst[r, 4, :], ALU.add).then_inc(weights, 1)
            pool.wait_ge(in_w2, 32)
            chain(pool.tensor_scalar(SW2, SW2, FINE, None, ALU.mult))
            chain(pool.tensor_copy(W2[:, 0], SW2))
            pool.tensor_tensor(W2[:, 1], SW2, W2[:, 0], ALU.subtract).then_inc(weights, 1)
            chain(pool.tensor_scalar(SB2[:, :], SB2[:, :], FINE, None, ALU.mult))
            chain(pool.tensor_copy(B2[:, 0], SB2[:, :]))
            pool.tensor_tensor(B2[:, 1], SB2[:, :], B2[:, 0], ALU.subtract).then_inc(weights, 1)
            chain(pool.memset(MASKK, MROW))
            for dst, value, keep in ((MASKQ, MASK[0], ALU.is_equal), (MASKK[0:8], MASK[1], ALU.not_equal)):
                chain(pool.memset(dst, value))
                sel = pool.affine_select(out=dst.rearrange("p (m c) -> p m c", m=8), in_=dst.rearrange("p (m c) -> p m c", m=8),
                                         compare_op=keep, fill=0.0, base=0, pattern=[[-1, 8], [0, 64]], channel_multiplier=1)
                chain(sel) if dst is MASKQ else sel.then_inc(att_const, 1)

        @block.tensor
        def _(pe):
            pe.wait_ge(consts, 1)
            pe.wait_ge(in_p, 48)
            for b, (r0, n) in enumerate(BLK):
                mm = pe.matmul(MISC[0:R, 0:R], PS[0:n, b, :], PS[0:n, b, :], start=(b == 0), stop=(b == 2))
            mm.then_inc(gram, 1)

            def filler(n, p_):
                f = FILL[n % 2]
                if p_ == 0 and n >= 2:
                    pe.wait_ge(fill_done, n - 1)
                if work[n] == "P'":
                    for b, (r0, k) in enumerate(BLK):
                        mm = pe.matmul(f[R * p_:R * p_ + R, r0:r0 + k], PS[0:k, b, :], ident[0:k, 0:k], start=True, stop=True)
                elif work[n] == "mod":
                    pe.wait_ge(fill_done, work.index("ada 0") + 1)
                    for b, (r0, k) in enumerate(BLK):
                        mm = pe.transpose(f[0:k, P * b:P * b + P], AD[:, 0, r0:r0 + k], ident[:, :])
                elif work[n][0] == "a":
                    if p_ == 0:
                        pe.wait_ge(in_ada, 48)
                        pe.wait_ge(in_adab, 16)
                        pe.wait_ge(silu, 1)
                    for j, v in enumerate(ADA_ROWS[int(work[n][-1])]):
                        o_, cols = f[32 * j:32 * j + 32, 0:D], slice(D * v, D * v + D)
                        if p_ < 3:
                            k = BLK[p_][1]
                            mm = pe.matmul(o_, SC32[0:k, p_, :], ADA[0:k, p_, cols], start=(p_ == 0), stop=False)
                        else:
                            mm = pe.matmul(o_, ones[0:1, 0:32], ADAB[:, cols], start=False, stop=True)
                elif work[n][1] < 3:
                    i, b = work[n]
                    if b == 0 and p_ == 0:
                        pe.wait_ge(in_x[i], 16)
                    r0, k = BLK[b]
                    mm = pe.transpose(f[0:k, P * p_:P * p_ + P], X[:, TPC * i + p_, r0:r0 + k], ident[:, :])
                else:
                    i = work[n][0]
                    if p_ == 0:
                        pe.wait_ge(fill_done, XDONE[i])
                    half, b = divmod(p_, 3)
                    r0, k = BLK[b]
                    for h in range(2):
                        c0 = CH * (i + 2 * h) + CH // 2 * half
                        mm = pe.matmul(f[R * h:R * h + R, CH // 2 * half:CH // 2 * (half + 1)], PS[0:k, b, :],
                                       XT[0:k, b, c0:c0 + CH // 2], start=(b == 0), stop=(b == 2))
                if pieces[last_piece[n]] == (n, p_):
                    mm.then_inc(fill_ready, 1)

            def gate(n):
                f = FILL[n % 2]
                pe.wait_ge(fill_done, max(n - 1, work.index("ada 1") + 1))
                g, b = divmod(n - FG, 2)
                row = 32 * g + b
                pe.matmul(f[:, 0:D], ident[0:R, row:row + 1].broadcast_to([R, P]), AD[0:R, 1, :], start=True, stop=True).then_inc(fill_ready, 1)

            def skew_matrix():
                pe.wait_ge(consts, 2)
                pe.wait_ge(up_in, 16 * (R - 1))
                for b in range(B):
                    o_ = EXPM[R * b:R * b + R, 0:R]
                    pe.matmul(o_, ident[0:R, 0:R], UP[:, b, :], start=True, stop=False)
                    mm = pe.matmul(o_, UP[:, b, :], NEGI[:, :], start=False, stop=True)
                mm.then_inc(skew_psum, 1)

            def exp_step(n):
                if n == 0:
                    pe.wait_ge(skew_ready, 2)
                pe.wait_ge(exp_sb, n + 1)
                src = YY[:, n % 2, :]
                for h in range(2):
                    cols = slice(R * h, R * h + R)
                    for b in range(B):
                        g = slice(R * b, R * b + R)
                        lhs = (XX if n < 3 else src)[g, R - R * h:2 * R - R * h]
                        mm = pe.matmul(EXPM[g, cols], lhs, src[g, cols], start=True, stop=True)
                mm.then_inc(exp_psum, 1)

            for k in range(R + LAG):
                if k < R:
                    pe.wait_ge(g_new, k + 1)
                    if k >= 2:
                        pe.wait_ge(row_ready, k - 1)
                    pe.matmul(PIV[k % 2][0:R, k:R + k + 1], ident[0:R, k:k + 1].broadcast_to([R, R]), G[:, k:R + k + 1],
                              start=True, stop=True).then_inc(piv_row, 1)
                own = pieces[max(0, PER * (k - FIRST)):max(0, PER * (k - FIRST + 1))]
                if 0 <= k - EXP_AT - 3 < NEXP:
                    exp_step(k - EXP_AT - 3)
                for n, p_ in own[:1]:
                    filler(n, p_)
                j = k - LAG
                if 0 <= j < R - 1:
                    one = ident[0:R, j:j + 1].broadcast_to([R, R])
                    pe.wait_ge(row_ready, j + 1)
                    pe.matmul(AROW[j % 2][0:R, j:R], one, ROWS[:, j % 4, j:R], start=True, stop=False)
                    pe.wait_ge(a_new, j + 1)
                    pe.matmul(AROW[j % 2][0:R, j:R], NEGI[:, j:j + 1].broadcast_to([R, R]), A[:, j:R], start=False, stop=False)
                    pe.wait_ge(a_sign, j + 1)
                    pe.matmul(AROW[j % 2][0:R, j:R], SG[:, j:j + 1].broadcast_to([R, R]), A[:, j:R],
                              start=False, stop=True).then_inc(a_row, 1)
                for n, p_ in own[1:]:
                    filler(n, p_)
                if k == EXP_AT:
                    skew_matrix()

            pe.wait_ge(basis, 2)
            pe.wait_ge(exp_sb, NEXP + 1)
            last = YY[:, NEXP % 2, :]
            for b in range(B):
                g = slice(R * b, R * b + R)
                mm = pe.matmul(EXPM[g, 0:R], last[g, R:2 * R], V2[g, :], start=True, stop=True)
            mm.then_inc(rot_psum, 1)
            pe.wait_ge(rot_sb, 1)
            for b in range(B):
                g = slice(R * b, R * b + R)
                mm = pe.matmul(MISC[g, 0:R], T1[g, :], V2[g, :], start=True, stop=True)
            mm.then_inc(rot_psum, 1)
            pe.wait_ge(rot_sb, 2)
            for b in range(B):
                g = slice(R * b, R * b + R)
                mm = pe.matmul(PIV[0][g, 0:D], NTs[g, :], PT2[g, :], start=True, stop=True)
            mm.then_inc(rot_psum, 1)
            for n in range(FG, NFILL):
                gate(n)
            pe.wait_ge(rot_sb, 3)
            pe.wait_ge(fill_done, NFILL)
            for t in range(NT):
                if t >= 2:
                    pe.wait_ge(x_rot, t - 1)
                b, a = divmod(t, 8)
                g = slice(R * b, R * b + R)
                pe.matmul(FILL[t % 2][:, 0:D], ZT[g, P * a:P * a + P], ROT[g, :], start=True, stop=True).then_inc(delta_ready, 1)

            def turn(n):
                pe.wait_ge(xn_ready, n + 1)
                for b, (r0, k) in enumerate(BLK):
                    if 3 * n + b >= 2:
                        pe.wait_ge(t32_ready, 3 * n + b - 1)
                    f = TRB[(3 * n + b) % 2]
                    for j in range(TPC):
                        rows = 96 if b == 2 else P
                        mm = pe.transpose(f[0:rows, P * j:P * j + P], XN[:, n % 2, j, r0:r0 + rows], ident[:, :])
                    mm.then_inc(tr_ready, 1)

            def qkv(n):
                pe.wait_ge(split_done, 3 * n + 3)
                if n == 0:
                    pe.wait_ge(weights, 2)
                for m, (f0, k) in enumerate(MT):
                    idx = NQ * n + m
                    if idx >= 2:
                        pe.wait_ge(qk_low, idx - 1)
                    for p_, (a_, w_, r) in enumerate(PARTS):
                        mm = pe.matmul(QB[idx % 2][0:k, :], WQ[0:r, w_, f0:f0 + k], HT[0:r, n % 2, a_, :], start=(p_ == 0), stop=(p_ == 6))
                    mm.then_inc(qk_ready, 1)

            turn(0)
            for n in range(NCH):
                if n + 1 < NCH:
                    turn(n + 1)
                qkv(n)

            def maxima(s_):
                n, u = divmod(s_, 16)
                if u == 0:
                    pe.wait_ge(qk_in[n], 96)
                    pe.wait_ge(att_rows[n // 2], 64)
                if s_ >= 2:
                    pe.wait_ge(mx_used, s_ - 1)
                for g in range(4):
                    mm = pe.matmul(MXB[s_ % 2][:, P * g:P * g + P], operand(n, 0, u, g, MROWS), operand(n, 1, u, g, MROWS),
                                   start=True, stop=True)
                mm.then_inc(mx_ready, 1)

            def scores(s_):
                n, u = divmod(s_, 16)
                if u == 0:
                    pe.wait_ge(max_in[n], 16)
                if s_ >= 2:
                    pe.wait_ge(exp_done, s_ - 1)
                for g in range(4):
                    mm = pe.matmul(SB[s_ % 2][:, P * g:P * g + P], operand(n, 1, u, g, MROWS + 1), operand(n, 0, u, g, MROWS + 1),
                                   start=True, stop=True)
                mm.then_inc(s_ready, 1)

            def v_groups(w):
                n, q = divmod(w, 4)
                r = R * (n % 2)
                if q == 0:
                    pe.wait_ge(v_in[n], 32)
                if w:
                    pe.wait_ge(vg_ready, w)
                for g in range(16):
                    mm = pe.matmul(VB[:, DH * g:DH * g + DH], VT[r:r + 2 * DH, 16 * q + g:16 * q + g + 64 * P - 63:64], SELV[r:r + 2 * DH, :],
                                   start=True, stop=True)
                mm.then_inc(vg_psum, 1)

            def values(s_):
                w, q = divmod(s_, 4)
                pe.wait_ge(exp_done, s_ + 1)
                if q == 0:
                    pe.wait_ge(vg_ready, w + 1)
                    if w >= 2:
                        pe.wait_ge(o_norm, w - 1)
                for g in range(4):
                    mm = pe.matmul(PO[w % 2][:, (DH + 1) * (4 * q + g):(DH + 1) * (4 * q + g + 1)], E[:, s_ % 3, P * g:P * g + P],
                                   VG[:, w % 2, 4 * q + g, :], start=True, stop=True)
                mm.then_inc(pv_ready, 1)

            pe.wait_ge(t32_ready, 3 * NCH)
            pe.wait_ge(qk_low, NQ * NCH)
            for s_ in range(UNITS + LEAD + BEHIND):
                st = s_ - LEAD
                if st == -1:
                    v_groups(0)
                if s_ < UNITS:
                    maxima(s_)
                if 0 <= st < UNITS:
                    scores(st)
                if st >= BEHIND:
                    values(st - BEHIND)
                    if st % 4 == 2 and st // 4 + 1 < UNITS // 4:
                        v_groups(st // 4 + 1)

            def project(n):
                pe.wait_ge(split_done, 3 * n + 3)
                if n == NCH:
                    pe.wait_ge(weights, 4)
                for j in range(TPC):
                    t = TPC * (n - NCH) + j
                    if t >= 2:
                        pe.wait_ge(proj_mul, t - 1)
                    for p_, (a_, w_, r) in enumerate(PARTS):
                        mm = pe.matmul(QB[t % 2][:, 0:D], HT[0:r, n % 2, a_, P * j:P * j + P], WP[0:r, w_, :], start=(p_ == 0), stop=(p_ == 6))
                    mm.then_inc(proj_ready, 1)

            turn(NCH)
            for n in range(NCH, 2 * NCH):
                if n + 1 < 2 * NCH:
                    turn(n + 1)
                project(n)

            def fc1(n):
                pe.wait_ge(split_done, 3 * n + 3)
                if n == 2 * NCH:
                    pe.wait_ge(weights, 6)
                for m in range(NF):
                    idx = NF * (n - 2 * NCH) + m
                    if idx >= 3:
                        pe.wait_ge(gelu_sb, idx - 2)
                    for p_, (a_, w_, r) in enumerate(PARTS):
                        mm = pe.matmul(FB[idx % 3], W1[0:r, w_, P * m:P * m + P], HT[0:r, n % 2, a_, :], start=(p_ == 0), stop=(p_ == 6))
                    mm.then_inc(fc1_ready, 1)

            def fc2(n):
                c_ = n - 2 * NCH
                pe.wait_ge(g_low, NF * (c_ + 1))
                if c_ == 0:
                    pe.wait_ge(weights, 8)
                g = GT[c_ % 2]
                for j in range(TPC):
                    t = TPC * c_ + j
                    if t >= 2:
                        pe.wait_ge(y_mul, t - 1)
                    cols = slice(P * j, P * j + P)
                    for half in range(2):
                        pe.matmul(YB[t % 2][:, 0:D], FOUR[:, :], B2[:, half, :], start=(half == 0), stop=False)
                    for f in range(NF):
                        for a_, w_ in ((0, 0), (1, 0), (0, 1)):
                            mm = pe.matmul(YB[t % 2][:, 0:D], g[:, a_, f, cols], W2[:, w_, f, :], start=False, stop=(f == NF - 1 and w_ == 1))
                    mm.then_inc(fc2_ready, 1)

            turn(2 * NCH)
            for n in range(2 * NCH, 3 * NCH):
                if n + 1 < 3 * NCH:
                    turn(n + 1)
                fc1(n)
                if n > 2 * NCH:
                    fc2(n - 1)
            fc2(3 * NCH - 1)

        @block.scalar
        def _(act):
            act.wait_ge(in_c, 48)
            act.activation(SC[:, 0], CT[:, :, :], ACT.Exp, scale=-1.0).then_inc(silu_e, 1)

            act.wait_ge(in_cb, 16)
            act.activation(SCB[:, 0], CB, ACT.Exp, scale=-1.0).then_inc(cb_e, 1)
            act.wait_ge(cb_e, 1)
            act.activation(SCB[:, 1], SCB[:, 0], ACT.Copy, bias=1.0).then_inc(cb_e, 1)

            def fill_out(n):
                act.wait_ge(fill_ready, n + 1)
                f = FILL[n % 2]
                if n >= FG:
                    g, b = divmod(n - FG, 2)
                    cp = act.mul(GATE[:, g, b, :], f[:, 0:D], 1.0 / (FINE * FINE))
                elif work[n] == "P'":
                    cp = act.copy(PT2[:, :], f[:, 0:D])
                elif work[n] == "mod":
                    act.wait_ge(consts, 2)
                    fv = f[:, 0:3 * P].rearrange("p (m v b) -> p v m b", m=3, v=4)[:, :, :, 0:B]
                    for q in range(2):
                        cp = act.activation(MOD[:, q:4:2, 0:2, :], fv[:, q:4:2, 0:2, :], ACT.Copy, scale=FINE, bias=FINE * q)
                        for rep in range(3):
                            cp = act.activation(MOD[32 * rep:32 * rep + 32, q:4:2, 2, :], fv[0:32, q:4:2, 2, :], ACT.Copy, scale=FINE, bias=FINE * q)
                            if rep < 2 or q == 0:
                                cp.then_inc(mod_part, 1)
                elif work[n][0] == "a":
                    g = int(work[n][-1])
                    rows = 32 * len(ADA_ROWS[g])
                    cp = act.copy(AD[0:rows, g, :], f[0:rows, 0:D])
                else:
                    i, b = work[n]
                    if b < 3:
                        k = BLK[b][1]
                        cp = act.copy(XT[0:k, b, CH * i:CH * i + CH], f[0:k, :])
                    else:
                        cp = act.copy(ZT[:, CH * i:CH * i + CH], f[:, :])
                cp.then_inc(fill_done, 1)

            for k in range(R + LAG + 1):
                if k < R - 1:
                    act.wait_ge(piv_inv, k + 1)
                    act.activation(RHO[:, k:k + 1], RI[:, k:k + 1], ACT.Sqrt, scale=1.0).then_inc(rho_ready, 1)
                    act.wait_ge(rho_ready, k + 1)
                    act.wait_ge(g_new, k + 2)
                    if k >= 4:
                        act.wait_ge(a_new, k - 2)
                    act.activation(ROWS[:, k % 4, k:R], PIV[k % 2][0:R, k:R], ACT.Copy, scale=RHO[:, k:k + 1]).then_inc(row_ready, 1)
                for n, i in last_piece.items():
                    if FIRST + i // PER == k - 1:
                        fill_out(n)
                if k == EXP_AT:
                    act.wait_ge(skew_psum, 1)
                    for h in range(2):
                        act.mul(XX[:, R * h:R * h + R], EXPM[:, 0:R], (1 - 2 * h) * 2.0 ** -SQUARINGS).then_inc(skew_ready, 1)
            act.wait_ge(diag, 2)
            act.activation(dg[:, 2:3], dg[:, 0:1], ACT.Sqrt, scale=1.0).then_inc(root, 1)

            for n in range(FG, NFILL):
                fill_out(n)

            def norm_root(l):
                act.wait_ge(stats, l + 1)
                act.activation(ST[:, l, 1, :], ST[:, l, 0, :], ACT.Sqrt).then_inc(root2, 1)

            def turn_out(n, l):
                for b in range(3):
                    idx = 3 * n + b
                    act.wait_ge(tr_ready, idx + 1)
                    if idx >= 2:
                        act.wait_ge(split_done, idx - 1)
                    rows = 96 if b == 2 else P
                    batch = (n % NCH) // 2
                    src, dst = TRB[idx % 2][0:rows, :], T32[0:rows, idx % 2, :]
                    if l == 0:
                        src = src.rearrange("p (a m v) -> p a m v", a=TPC, m=8)
                        dst = dst.rearrange("p (m a v) -> p a m v", a=TPC, m=8)
                    if l is None:
                        cp = act.mul(dst, src, FINE)
                    else:
                        cp = act.activation(dst, src, ACT.Identity,
                                            scale=MOD[0:rows, 2 * l + 1, b, batch:batch + 1], bias=MOD[0:rows, 2 * l, b, batch:batch + 1])
                    cp.then_inc(t32_ready, 1)

            def qkv_out(n):
                for m, (f0, k) in enumerate(MT):
                    idx = NQ * n + m
                    act.wait_ge(qk_ready, idx + 1)
                    if idx >= 4:
                        act.wait_ge(qk_out[idx % 4], 16 * (idx // 4))
                    act.mul(QS[0:k, idx % 4, 0, :], QB[idx % 2][0:k, :], QSCALE / (FINE * FINE)).then_inc(qk_high, 1)

            norm_root(0)
            turn_out(0, 0)
            for n in range(NCH):
                if n + 1 < NCH:
                    turn_out(n + 1, 0)
                qkv_out(n)

            def exponentials(s_):
                act.wait_ge(s_ready, s_ + 1)
                if s_ >= 3:
                    act.wait_ge(pv_ready, s_ - 2)
                act.activation(E[:, s_ % 3, :], SB[s_ % 2], ACT.Exp, scale=DH ** -0.5 / (QSCALE * QSCALE)).then_inc(exp_done, 1)

            def v_out(w):
                act.wait_ge(vg_psum, w + 1)
                if w >= 2:
                    act.wait_ge(pv_ready, 4 * w - 4)
                act.mul(VG[:, w % 2, :, 0:DH], VB[:, 0:16 * DH].rearrange("p (g d) -> p g d", g=16), 1.0 / QSCALE).then_inc(vg_ready, 1)

            v_out(0)
            for st in range(UNITS):
                exponentials(st)
                if st >= BEHIND and st % 4 == 2 and st // 4 + 1 < UNITS // 4:
                    v_out(st // 4 + 1)

            turn_out(NCH, None)
            for n in range(NCH, 2 * NCH):
                if n + 1 < 2 * NCH:
                    turn_out(n + 1, None)
            norm_root(1)

            def gelu(n):
                for m in range(NF):
                    idx = NF * (n - 2 * NCH) + m
                    act.wait_ge(fc1_ready, idx + 1)
                    if idx >= 2:
                        act.wait_ge(g_low, idx - 1)
                    act.activation(G32[:, idx % 2, :], FB[idx % 3], ACT.Gelu, scale=1.0 / (FINE * FINE)).then_inc(gelu_sb, 1)

            turn_out(2 * NCH, 1)
            for n in range(2 * NCH, 3 * NCH):
                if n + 1 < 3 * NCH:
                    turn_out(n + 1, 1)
                gelu(n)

        @block.vector
        def _(dve):
            dve.wait_ge(gram, 1)
            dve.wait_ge(consts, 1)
            dve.tensor_copy(G[:, 0:R], MISC[0:R, 0:R]).then_inc(g_new, 1)
            dve.tensor_copy(A[:, :], PS[0:R, 0, :]).then_inc(a_new, 1)
            dve.wait_ge(g_new, 1)
            dve.wait_ge(a_new, 1)

            def silu_cond():
                dve.wait_ge(silu_e, 1)
                dve.tensor_scalar(SC[:, 1], SC[:, 0], 1.0, None, ALU.add).then_inc(silu_e, 1)
                dve.wait_ge(silu_e, 2)
                dve.reciprocal(SC[:, 2], SC[:, 1]).then_inc(silu_e, 1)
                dve.wait_ge(silu_e, 3)
                dve.tensor_tensor(SC32[:, :, 0:B], SC[:, 2], CT[:, :, :], ALU.mult).then_inc(silu, 1)

            def silu_rows():
                dve.wait_ge(cb_e, 2)
                dve.reciprocal(SCB[:, 2], SCB[:, 1]).then_inc(cb_e, 1)
                dve.wait_ge(cb_e, 3)
                dve.tensor_tensor(SCB[:, 2], SCB[:, 2], CB, ALU.mult).then_inc(cb_done, 1)

            def skew_entries(t):
                if t == 0:
                    dve.wait_ge(in_w, 16)
                    dve.wait_ge(cb_done, 1)
                for b in range(B):
                    n = B * t + b
                    if n >= 4:
                        dve.wait_ge(v_sum, n - 3)
                    dve.tensor_tensor_reduce(JUNK[:, n % 4, :], WL[:, t, :], SCB[:, 2, b, :], 1.0, 0.0, ALU.mult, ALU.add,
                                             VR[:, 0, b, t:t + 1]).then_inc(v_sum, 1)

            def sign(j):
                dve.scalar_tensor_tensor(out=SG[:, j:j + 1], in0=A[:, j:j + 1], scalar=0.0, in1=TWO[0:R, j:j + 1],
                                         op0=ALU.is_ge, op1=ALU.mult).then_inc(a_sign, 1)

            def exp_out(n):
                dst = YY[:, (n + 1) % 2, :]
                if n == -1:
                    dve.wait_ge(skew_ready, 2)
                    op = dve.scalar_tensor_tensor(out=dst, in0=XX[:, :], scalar=0.25, in1=II[:, :], op0=ALU.mult, op1=ALU.add)
                else:
                    dve.wait_ge(exp_psum, n + 1)
                    if n < 2:
                        op = dve.scalar_tensor_tensor(out=dst, in0=EXPM[:, 0:2 * R], scalar=1.0 / (3 - n), in1=II[:, :], op0=ALU.mult, op1=ALU.add)
                    elif n == 2:
                        op = dve.tensor_copy(dst, EXPM[:, 0:2 * R])
                    else:
                        dve.wait_ge(exp_sb, n + 1)
                        op = dve.scalar_tensor_tensor(out=dst, in0=YY[:, n % 2, :], scalar=2.0, in1=EXPM[:, 0:2 * R], op0=ALU.mult, op1=ALU.add)
                op.then_inc(exp_sb, 1)

            dve.wait_ge(consts, 2)
            sign(0)
            for k in range(R + LAG):
                j = k - LAG
                if k < R:
                    dve.wait_ge(piv_row, k + 1)
                    dve.reciprocal(RI[:, k:k + 1], PIV[k % 2][0:R, k:k + 1]).then_inc(piv_inv, 1)
                if k < R - 1:
                    dve.wait_ge(piv_inv, k + 1)
                    dve.tensor_scalar(CG[:, k:k + 1], G[:, k:k + 1], RI[:, k:k + 1], below[:, k:k + 1], ALU.mult, ALU.mult).then_inc(gcoef, 1)
                    dve.wait_ge(gcoef, k + 1)
                    dve.scalar_tensor_tensor(out=G[:, k + 1:R + k + 1], in0=PIV[k % 2][0:R, k + 1:R + k + 1], scalar=CG[:, k:k + 1],
                                             in1=G[:, k + 1:R + k + 1], op0=ALU.mult, op1=ALU.add).then_inc(g_new, 1)
                if 0 <= j < R - 1:
                    dve.wait_ge(a_row, j + 1)
                    dve.reciprocal(RA[:, j:j + 1], AROW[j % 2][0:R, j:j + 1]).then_inc(a_piv, 1)
                    dve.wait_ge(a_piv, j + 1)
                    dve.tensor_scalar(CA[:, j:j + 1], A[:, j:j + 1], RA[:, j:j + 1], below[:, j:j + 1], ALU.mult, ALU.mult).then_inc(acoef, 1)
                    dve.wait_ge(acoef, j + 1)
                    dve.scalar_tensor_tensor(out=A[:, j + 1:R], in0=AROW[j % 2][0:R, j + 1:R], scalar=CA[:, j:j + 1],
                                             in1=A[:, j + 1:R], op0=ALU.mult, op1=ALU.add).then_inc(a_new, 1)
                    dve.wait_ge(a_new, j + 2)
                    sign(j + 1)
                if k == 2:
                    silu_cond()
                    silu_rows()
                if V_AT <= k < V_AT + WTILES:
                    skew_entries(k - V_AT)
                if k == V_AT + WTILES:
                    dve.wait_ge(v_sum, B * WTILES)
                    dve.wait_ge(in_br, 16)
                    dve.tensor_tensor(VR[:, 1], VR[:, 0], BR.unsqueeze(1).broadcast_to([WROWS, B, WTILES]), ALU.add).then_inc(v_all, 1)
                if -1 <= k - EXP_AT - 2 < NEXP:
                    exp_out(k - EXP_AT - 2)
            dve.wait_ge(a_sign, R)
            dve.wait_ge(piv_inv, R)
            for n, src in ((0, RI), (1, SG)):
                dve.tensor_tensor_reduce(DJ[:, n, :], src[:, :], ident[0:R, 0:R], 1.0, 0.0, ALU.mult, ALU.add, dg[:, n:n + 1]).then_inc(diag, 1)
            dve.wait_ge(root, 1)
            dve.wait_ge(diag, 2)
            dve.reciprocal(dg[:, 3:4], dg[:, 2:3]).then_inc(root, 1)
            dve.wait_ge(root, 2)
            dve.tensor_scalar(dg[:, 4:5], dg[:, 3:4], dg[:, 0:1], dg[:, 2:3], ALU.mult, ALU.add).then_inc(root, 1)
            dve.tensor_scalar(dg[:, 5:6], dg[:, 1:2], 0.5, 0.5, ALU.mult, ALU.subtract).then_inc(root, 1)
            dve.wait_ge(root, 4)
            dve.wait_ge(g_new, R)
            for g in range(2):
                dve.tensor_scalar(V2[R * g:R * g + R, :], G[:, R:2 * R], dg[:, 4:5], dg[:, 5:6], ALU.mult, ALU.mult).then_inc(basis, 1)
            dve.wait_ge(rot_psum, 1)
            dve.tensor_copy(T1[:, :], EXPM[:, 0:R]).then_inc(rot_sb, 1)
            dve.wait_ge(rot_psum, 2)
            dve.tensor_copy(NTs[:, :], MISC[:, 0:R]).then_inc(rot_sb, 1)
            dve.wait_ge(rot_psum, 3)
            dve.tensor_copy(ROT[:, :], PIV[0][:, 0:D]).then_inc(rot_sb, 1)
            def stat(l, t):
                idx = NT * l + t
                if t >= 2 or l:
                    dve.wait_ge(bn_s, 2 * idx - 2)
                dve.bn_stats(BN[:, t % 2, :], X[:, t, :]).then_inc(bn_s, 1)
                dve.wait_ge(bn_s, 2 * idx + 1)
                dve.bn_aggr(MV[:, l, t, :], BN[:, t % 2, :]).then_inc(bn_s, 1)

            def norm_scales(l):
                s_ = ST[:, l]
                n0 = 5 * l
                dve.wait_ge(bn_s, 2 * NT * (l + 1))
                dve.tensor_scalar(s_[:, 0, :], MV[:, l, :, 1], EPS, None, ALU.add).then_inc(stats, 1)
                dve.wait_ge(root2, l + 1)
                dve.wait_ge(stats, l + 1)
                dve.reciprocal(s_[:, 2, :], s_[:, 1, :]).then_inc(scales, 1)
                dve.wait_ge(scales, n0 + 1)
                dve.tensor_tensor(s_[:, 3, :], s_[:, 2, :], s_[:, 2, :], ALU.mult).then_inc(scales, 1)
                dve.wait_ge(scales, n0 + 2)
                dve.tensor_tensor(s_[:, 4, :], s_[:, 3, :], s_[:, 0, :], ALU.mult).then_inc(scales, 1)
                dve.wait_ge(scales, n0 + 3)
                dve.tensor_scalar(s_[:, 5, :], s_[:, 4, :], -0.5, 1.5, ALU.mult, ALU.add).then_inc(scales, 1)
                dve.wait_ge(scales, n0 + 4)
                dve.tensor_tensor(s_[:, 6, :], s_[:, 5, :], s_[:, 2, :], ALU.mult).then_inc(scales, 1)
                dve.wait_ge(scales, n0 + 5)

            def source(n, l):
                if n >= 2:
                    dve.wait_ge(tr_ready, 3 * n - 3)
                for j in range(TPC):
                    t = TPC * (n % NCH) + j
                    if l is None:
                        dve.tensor_copy(XN[:, n % 2, j, 0:D], stage[:, D * t:D * t + D]).then_inc(xn_main, 1)
                    else:
                        dve.tensor_scalar(XN[:, n % 2, j, 0:D], X[:, t, :], MV[:, l, t, 0:1], ST[:, l, 6, t:t + 1],
                                          ALU.subtract, ALU.mult).then_inc(xn_main, 1)
                dve.wait_ge(xn_main, TPC * (n + 1))
                dve.tensor_copy(XN[:, n % 2, :, D:DX].rearrange("p t (a c) -> p t a c", a=2),
                                XN[:, n % 2, :, D - 32:D].unsqueeze(2).broadcast_to([P, TPC, 2, 32])).then_inc(xn_ready, 1)

            def split(n):
                for b in range(3):
                    idx = 3 * n + b
                    dve.wait_ge(t32_ready, idx + 1)
                    if b == 0 and n >= 2:
                        if n < NCH:
                            dve.wait_ge(qk_ready, NQ * (n - 1))
                        elif NCH + 2 <= n < 2 * NCH:
                            dve.wait_ge(proj_ready, TPC * (n - NCH - 1))
                        elif n >= 2 * NCH + 2:
                            dve.wait_ge(fc1_ready, NF * (n - 2 * NCH - 1))
                        elif n >= 2 * NCH:
                            dve.wait_ge(proj_ready, TPC * (n - NCH - 1))
                    rows = slice(0, 96) if b == 2 else slice(0, P)
                    high = HT[rows, n % 2, 4 if b == 2 else b, :]
                    dve.tensor_copy(high, T32[rows, idx % 2, :]).then_inc(cast_done, 1)
                    dve.wait_ge(cast_done, idx + 1)
                    rows = slice(32, 64) if b == 2 else slice(0, P)
                    low = HT[rows, n % 2, 4 if b == 2 else 2 + b, :]
                    high = HT[rows, n % 2, 4 if b == 2 else b, :]
                    dve.tensor_tensor(low, T32[rows, idx % 2, :], high, ALU.subtract).then_inc(split_done, 1)

            def ones_rows(n):
                for a_ in range(2):
                    dve.memset(HT[96:P, a_, 4, :], FINE).then_inc(ht_ones, 1)
                dve.wait_ge(ht_ones, 2 * n + 2)

            for t in range(NT):
                dve.wait_ge(delta_ready, t + 1)
                dve.tensor_tensor(X[:, t, :], FILL[t % 2][:, 0:D], X[:, t, :], ALU.add).then_inc(x_rot, 1)
                if t >= 1:
                    dve.wait_ge(x_rot, t)
                    stat(0, t - 1)
            dve.wait_ge(x_rot, NT)
            stat(0, NT - 1)
            norm_scales(0)
            dve.wait_ge(fill_done, NFILL)
            ones_rows(0)
            source(0, 0)
            source(1, 0)
            split(0)
            for n in range(NCH):
                if n + 1 < NCH:
                    split(n + 1)
                for m, (f0, k) in enumerate(MT):
                    idx = NQ * n + m
                    dve.wait_ge(qk_high, idx + 1)
                    dve.scalar_tensor_tensor(out=QS[0:k, idx % 4, 1, :], in0=QB[idx % 2][0:k, :], scalar=QSCALE / (FINE * FINE),
                                             in1=QS[0:k, idx % 4, 0, :], op0=ALU.mult, op1=ALU.subtract).then_inc(qk_low, 1)
                if n + 2 < NCH:
                    source(n + 2, 0)

            def maximum(s_):
                n, u = divmod(s_, 16)
                dve.wait_ge(mx_ready, s_ + 1)
                dve.tensor_reduce(MX[:, n, 4 * u:4 * u + 4], MXB[s_ % 2].rearrange("p (g c) -> p g c", g=4), AX.X, ALU.max,
                                  negate=True).then_inc(mx_used, 1)
                if u == 15:
                    dve.wait_ge(mx_used, s_ + 1)
                    dve.tensor_scalar(MR[:, n, :], MX[:, n, :], 1.0 / MROW, None, ALU.mult).then_inc(mx_half, 1)

            def normalise(w):
                n, q = divmod(w, 4)
                dve.wait_ge(pv_ready, 4 * w + 4)
                if w == 0:
                    dve.wait_ge(weights, 8)
                if w >= 2:
                    dve.wait_ge(o_norm, w - 1)
                po = PO[w % 2][:, 0:16 * (DH + 1)].rearrange("p (g d) -> p g d", g=16)
                dve.reciprocal(RD[:, w % 2, :], po[:, :, DH]).then_inc(o_sum, 1)
                dve.wait_ge(o_sum, w + 1)
                dve.tensor_tensor(AO[:, n // 2, :, :, 4 * (n % 2) + q, :],
                                  po[:, :, 0:DH].rearrange("p (a e) d -> p a e d", e=2),
                                  RD[:, w % 2, :].rearrange("p (a e) -> p a e", e=2).unsqueeze(3).broadcast_to([P, 8, 2, DH]),
                                  ALU.mult).then_inc(o_norm, 1)

            for s_ in range(UNITS + LEAD + BEHIND):
                if s_ < UNITS:
                    maximum(s_)
                k = s_ - LEAD - BEHIND - 3
                if k >= 0 and k % 4 == 0:
                    normalise(k // 4)
            dve.wait_ge(o_norm, UNITS // 4)
            source(NCH, None)
            source(NCH + 1, None)
            split(NCH)
            for n in range(NCH, 2 * NCH):
                if n + 1 < 2 * NCH:
                    split(n + 1)
                for j in range(TPC):
                    t = TPC * (n - NCH) + j
                    dve.wait_ge(proj_ready, t + 1)
                    if t >= 6:
                        dve.wait_ge(x_mid, t - 5)
                    dve.tensor_tensor(YT[:, t % 6, :], QB[t % 2][:, 0:D], GATE[:, 0, t // 8, :], ALU.mult).then_inc(proj_mul, 1)
                    dve.wait_ge(proj_mul, t + 1)
                    dve.tensor_tensor(X[:, t, :], X[:, t, :], YT[:, t % 6, :], ALU.add).then_inc(x_mid, 1)
                    dve.wait_ge(x_mid, t + 1)
                    stat(1, t)
                if n + 2 < 2 * NCH:
                    source(n + 2, None)
            norm_scales(1)
            source(2 * NCH, 1)
            source(2 * NCH + 1, 1)
            split(2 * NCH)

            def gelu_split(n):
                c_ = n - 2 * NCH
                for m in range(NF):
                    idx = NF * c_ + m
                    dve.wait_ge(gelu_sb, idx + 1)
                    if m == 0 and c_ >= 2:
                        dve.wait_ge(fc2_ready, TPC * (c_ - 1))
                    dve.tensor_scalar(GT[c_ % 2][:, 0, m, :], G32[:, idx % 2, :], FINE, None, ALU.mult).then_inc(g_high, 1)
                    dve.wait_ge(g_high, idx + 1)
                    dve.scalar_tensor_tensor(out=GT[c_ % 2][:, 1, m, :], in0=G32[:, idx % 2, :], scalar=FINE,
                                             in1=GT[c_ % 2][:, 0, m, :], op0=ALU.mult, op1=ALU.subtract).then_inc(g_low, 1)

            def result(n):
                for j in range(TPC):
                    t = TPC * (n - 2 * NCH) + j
                    dve.wait_ge(fc2_ready, t + 1)
                    if t >= 6:
                        dve.wait_ge(y_out[t % 6], 16 * (t // 6))
                    dve.tensor_tensor(YT[:, t % 6, :], YB[t % 2][:, 0:D], GATE[:, 1, t // 8, :], ALU.mult).then_inc(y_mul, 1)
                    dve.wait_ge(y_mul, t + 1)
                    dve.tensor_tensor(YT[:, t % 6, :], YT[:, t % 6, :], X[:, t, :], ALU.add).then_inc(y_ready, 1)

            for n in range(2 * NCH, 3 * NCH):
                if n + 1 < 3 * NCH:
                    split(n + 1)
                gelu_split(n)
                if n + 2 < 3 * NCH:
                    source(n + 2, 1)
                if n > 2 * NCH:
                    result(n - 1)
            result(3 * NCH - 1)


_INS = ["x", "cond_1152", "L0_cond_P", "L0_cond_W", "L0_cond_b", "L1_cond_qkv_w", "L1_cond_qkv_b", "L1_cond_proj_w",
        "L1_cond_proj_b", "L1_cond_fc1_w", "L1_cond_fc1_b", "L1_cond_fc2_w", "L1_cond_fc2_b", "L1_cond_ada_w", "L1_cond_ada_b"]


def kernel(**inputs):
    import numpy as _np
    import concourse.bacc as _bacc
    from concourse import mybir as _mybir
    from concourse.bass_utils import run_bass_kernel_spmd as _run

    nc = _bacc.Bacc("TRN2", target_bir_lowering=False, num_devices=1)
    arrays, args = {}, []
    for name in _INS:
        a = _np.ascontiguousarray(inputs[name])
        arrays[f"in_{name}_dram"] = a
        args.append(nc.dram_tensor(f"in_{name}_dram", a.shape, _mybir.dt.from_np(a.dtype), kind="ExternalInput").ap())
    args.append(nc.dram_tensor("out_0_dram", (2, 1024, 288), _mybir.dt.float32, kind="ExternalOutput").ap())
    build(nc, *args)
    r = _run(nc, [arrays], core_ids=[0])
    return r.results[0]["out_0_dram"]
```

```python
from contextlib import ExitStack

import concourse.bass as bass
from concourse import mybir

F32 = mybir.dt.float32
F16 = mybir.dt.float16
ALU = mybir.AluOpType
ACT = mybir.ActivationFunctionType
AX = mybir.AxisListType

B, T, D = 2, 1024, 288
R = 64
H, DH = 16, 18
MLP = 4 * D
P = 128
NT = B * T // P
CH = 512
NCH = B * T // CH
TPC = CH // P
BLK = ((0, 128), (128, 128), (256, 32))
NF = MLP // P
NSKEW = R * (R - 1) // 2
WTILES = 16
WROWS = NSKEW // WTILES
SQUARINGS = 16
FINE = 64.0
EPS = 1e-6


def build(nc, x, c, pmat, wskew, bskew, qkv_w, qkv_b, proj_w, proj_b, fc1_w, fc1_b, fc2_w, fc2_b, ada_w, ada_b, out):
    with ExitStack() as ctx:
        def sb(name, shape, dt=F32):
            return ctx.enter_context(nc.sbuf_tensor(name, shape, dt))

        def sem(name):
            return ctx.enter_context(nc.semaphore(name))

        psum = ctx.enter_context(nc.psum_tensor("psum", [P, 8, 512], F32))
        bank = [psum[:, i, :] for i in range(8)]

        X = sb("X", [P, NT, D])
        big = sb("big", [P, 22528])
        WL = big[0:WROWS, 0:WTILES * D].rearrange("p (t n) -> p t n", t=WTILES)
        o = WTILES * D
        ZT = big[:, 0:T]
        ROT = big[:, T:T + D]
        AD = big[:, T + D:T + 3 * D].rearrange("p (g n) -> p g n", g=2)
        ADA = big[:, o:o + 18 * D].rearrange("p (b n) -> p b n", b=3)
        o += 18 * D
        SWP = big[:, o:o + 3 * D].rearrange("p (b n) -> p b n", b=3)
        o += 3 * D
        SW1 = big[:, o:o + 12 * D].rearrange("p (b n) -> p b n", b=3)
        o += 12 * D
        SCB = big[0:WROWS, o:o + 6 * D].rearrange("p (s b n) -> p s b n", s=3, b=B)
        o += 6 * D
        SB2 = big[0:1, o:o + D]
        assert o + D <= 22528 - 3 * B * T
        XT = big[:, 22528 - 3 * B * T:22528].rearrange("p (b t) -> p b t", b=3)
        stage = sb("stage", [P, 18 * D])
        SWQ = stage[:, 0:9 * D].rearrange("p (b n) -> p b n", b=3)
        SW2 = stage[:, 9 * D:18 * D].rearrange("p (b n) -> p b n", b=NF)
        CB = stage[0:WROWS, 9 * D:11 * D].rearrange("p (b n) -> p b n", b=B)
        JUNK = stage[0:WROWS, 11 * D:15 * D].rearrange("p (a n) -> p a n", a=4)
        WQ = sb("WQ", [P, 5, 3 * D], F16)
        WP = sb("WP", [P, 5, D], F16)
        W1 = sb("W1", [P, 5, MLP], F16)
        W2 = sb("W2", [P, 2, NF, D], F16)
        B2 = sb("B2", [1, 2, D], F16)
        GATE = sb("GATE", [P, 2, B, D])
        MOD = sb("MOD", [P, 4, 3, B])
        ident = sb("ident", [P, P])
        ones = sb("ones", [P, P])

        scratch = sb("scratch", [P, 9320])
        used = [0]

        def part(rows, *dims):
            n = 1
            for d in dims:
                n *= d
            a = scratch[0:rows, used[0]:used[0] + n]
            used[0] += n
            if len(dims) == 2:
                a = a.rearrange("p (a b) -> p a b", a=dims[0])
            if len(dims) == 3:
                a = a.rearrange("p (a b c) -> p a b c", a=dims[0], b=dims[1])
            return a

        VR = part(WROWS, 2, B, WTILES)
        BR = part(WROWS, WTILES)
        ADAB = part(1, 6 * D)
        SC32 = part(P, 3, 32)
        below = part(R, R)
        lowrow = sb("lowrow", [P, 1])
        TWO = part(P, P)
        II = part(P, P)
        PS = part(P, 3, R)
        PT2 = part(P, D)
        CT = part(P, 3, B)
        SC = part(P, 3, 3, B)
        G = part(R, 2 * R)
        A = part(R, R)
        RI = part(R, R)
        SG = part(R, R)
        RHO = part(R, R)
        ROWS = part(R, 4, R)
        CG = part(R, R)
        CA = part(R, R)
        RA = part(R, R)
        DJ = part(R, 2, R)
        dg = part(R, 8)
        V2 = part(P, R)
        UP = part(R, B, R)
        NEGI = part(R, R)
        XX = part(P, 2 * R)
        YY = part(P, 2, 2 * R)
        T1 = part(P, R)
        NTs = part(P, R)

        ST = sb("ST", [P, 2, 8, NT])
        MV = sb("MV", [P, 2, NT, 2])
        BN = sb("BN", [P, 2, 6])
        FOUR = sb("FOUR", [1, P], F16)
        SELV = sb("SELV", [P, DH], F16)
        MX = sb("MX", [P, NCH, 64])
        MR = sb("MR", [P, NCH, 64], F16)
        RD = sb("RD", [P, 2, 16])
        o = 0
        DX = D + 64
        XN = scratch[:, o:o + 2 * TPC * DX].rearrange("p (a t n) -> p a t n", a=2, t=TPC)
        o += 2 * TPC * DX
        T32 = scratch[:, o:o + 2 * CH].rearrange("p (a n) -> p a n", a=2)
        VG = scratch[:, o:o + 2 * CH].rearrange("p (a g d) -> p a g d", a=2, g=16)
        o += 2 * CH
        OT = [scratch[:, o + a_ * 5 * CH // 2:o + a_ * 5 * CH // 2 + CH] for a_ in range(2)]
        HT = scratch[:, o:o + 5 * CH].bitcast(F16).rearrange("p (a s n) -> p a s n", a=2, s=5)
        o += 5 * CH
        QS = scratch[:, o:o + 4 * CH].bitcast(F16).rearrange("p (a s n) -> p a s n", a=4, s=2)
        assert o + 4 * CH <= 9320
        QKT = [big[:, 14336:22528].bitcast(F16).rearrange("p (w c) -> p w c", w=2),
               big[:, 0:8192].bitcast(F16).rearrange("p (w c) -> p w c", w=2)]
        VT = big[:, 8192:12288].bitcast(F16)
        E = big[:, 12288:12288 + 3 * CH].rearrange("p (a n) -> p a n", a=3)
        CST = big[:, 12288 + 3 * CH:14336].bitcast(F16)
        MASKQ, MASKK = CST[0:8, 0:CH], CST[0:9, CH:2 * CH]
        AO = stage[:, 0:NT * D].rearrange("p (b a e c d) -> p b a e c d", b=B, a=8, e=2, c=8)
        GT = [big[:, 0:NF * CH].bitcast(F16).rearrange("p (s f n) -> p s f n", s=2, f=NF),
              big[:, NF * CH:2 * NF * CH].bitcast(F16).rearrange("p (s f n) -> p s f n", s=2, f=NF)]
        G32 = big[:, 2 * NF * CH:2 * NF * CH + 2 * CH].rearrange("p (a n) -> p a n", a=2)
        YT = big[:, 2 * (NF + 1) * CH:2 * (NF + 1) * CH + 6 * D].rearrange("p (a n) -> p a n", a=6)
        vd = nc.dram_tensor("skew_entries", [B, NSKEW], F32, kind="Internal").ap()
        qkd = nc.dram_tensor("qkv_halves", [2, NCH, 3 * D, CH], F16, kind="Internal").ap()

        in_p, in_c, in_cb, in_w, in_br, in_ada, in_adab = (sem(n) for n in ("in_p", "in_c", "in_cb", "in_w", "in_br", "in_ada", "in_adab"))
        in_wq, in_wp, in_w1, in_w2 = (sem(n) for n in ("in_wq", "in_wp", "in_w1", "in_w2"))
        in_x = [sem(f"in_x{i}") for i in range(NCH)]
        consts = sem("consts")
        pool_step = sem("pool_step")
        ct_clear = sem("ct_clear")
        silu_e = sem("silu_e")
        silu = sem("silu")
        cb_e, cb_done = sem("cb_e"), sem("cb_done")
        v_sum, v_all, v_out_done, up_clear, up_in = sem("v_sum"), sem("v_all"), sem("v_out_done"), sem("up_clear"), sem("up_in")
        gram = sem("gram")
        state0 = sem("state0")
        piv_row, piv_inv, gcoef, g_new = sem("piv_row"), sem("piv_inv"), sem("gcoef"), sem("g_new")
        rho_ready, row_ready = sem("rho_ready"), sem("row_ready")
        a_row, a_piv, acoef, a_new, a_sign = sem("a_row"), sem("a_piv"), sem("acoef"), sem("a_new"), sem("a_sign")
        fill_ready, fill_done = sem("fill_ready"), sem("fill_done")
        skew_psum, skew_ready = sem("skew_psum"), sem("skew_ready")
        exp_psum, exp_sb = sem("exp_psum"), sem("exp_sb")
        diag, root, basis = sem("diag"), sem("root"), sem("basis")
        rot_psum, rot_sb = sem("rot_psum"), sem("rot_sb")
        delta_ready, x_rot = sem("delta_ready"), sem("x_rot")
        weights = sem("weights")
        mod_part = sem("mod_part")
        bn_s, stats, root2, scales = sem("bn_s"), sem("stats"), sem("root2"), sem("scales")
        ht_ones = sem("ht_ones")
        xn_ready, tr_ready, t32_ready, cast_done, split_done = (
            sem(n) for n in ("xn_ready", "tr_ready", "t32_ready", "cast_done", "split_done"))
        qk_ready, qk_high, qk_low = sem("qk_ready"), sem("qk_high"), sem("qk_low")
        qk_out = [sem(f"qk_out{i}") for i in range(4)]
        att_const = sem("att_const")
        att_rows = [sem(f"att_rows{i}") for i in range(2)]
        qk_in = [sem(f"qk_in{i}") for i in range(NCH)]
        v_in = [sem(f"v_in{i}") for i in range(NCH)]
        max_in = [sem(f"max_in{i}") for i in range(NCH)]
        mx_ready, mx_used, mx_half = sem("mx_ready"), sem("mx_used"), sem("mx_half")
        s_ready, exp_done = sem("s_ready"), sem("exp_done")
        vg_psum, vg_ready, pv_ready, o_sum, o_norm = (sem(n) for n in ("vg_psum", "vg_ready", "pv_ready", "o_sum", "o_norm"))
        proj_ready, proj_mul, x_mid = sem("proj_ready"), sem("proj_mul"), sem("x_mid")
        fc1_ready, gelu_sb, g_high, g_low = sem("fc1_ready"), sem("gelu_sb"), sem("g_high"), sem("g_low")
        fc2_ready, y_mul, y_ready = sem("fc2_ready"), sem("y_mul"), sem("y_ready")
        y_out = [sem(f"y_out{i}") for i in range(6)]
        xn_main = sem("xn_main")
        vg_clear, ot_ready, o_turned = sem("vg_clear"), sem("ot_ready"), sem("o_turned")

        PIV = [bank[0], bank[1]]
        AROW = [bank[2], bank[5]]
        FILL = [bank[3], bank[4]]
        EXPM = bank[6]
        MISC = bank[7]

        work = ["P'", (0, 0), (0, 1), (0, 2), (2, 0), (2, 1), (2, 2), (1, 0), (0, 3), (1, 1), (1, 2), (3, 0), (3, 1), (3, 2),
                "ada 0", "ada 1", (1, 3), "mod"]
        ADA_ROWS = ((0, 1, 3, 4), (2, 5))
        FG = len(work)
        NFILL = FG + 4
        XDONE = [work.index((i + 2, 2)) + 1 for i in range(2)]
        pieces = []
        for n, w in enumerate(work):
            pieces += [(n, p_) for p_ in range({"P'": 2, "mod": 1}.get(w, 4 if w[0] == "a" else 6 if w[1] == 3 else 4))]
        last_piece = {n: i for i, (n, _) in enumerate(pieces)}
        FIRST = 5
        PER = 2
        V_AT = 4
        V_PER = 2
        EXP_AT = 43
        NEXP = 3 + SQUARINGS
        LAG = 2
        assert FIRST + len(pieces) // PER < R + LAG and EXP_AT + NEXP + 2 < R + LAG

        TURN1_AT = 4
        TURN_AT = 2

        def modulated(n):
            return n if n < NCH else n - NCH
        TRB = [bank[0], bank[1]]
        QB = [bank[2], bank[5], bank[6]]
        MXB, SB, VB, PO, OB = [bank[3], bank[4]], [bank[0], bank[1]], bank[2], [bank[5], bank[6]], bank[7]
        FB = [bank[2], bank[3], bank[4]]
        YB = [bank[5], bank[6]]
        PARTS = ((0, 0, P), (1, 1, P), (2, 0, P), (3, 1, P), (0, 2, P), (1, 3, P), (4, 4, 98))
        MT = [(126 * m, min(126, 3 * D - 126 * m)) for m in range(7)]
        NQ = len(MT)
        UNITS = 16 * NCH
        QSCALE = 8.0
        MROW = 16.0
        MASK = (240.0, -60000.0)
        HALVES = 3 * DH
        MROWS = HALVES + 8
        LEAD = 32
        AHEAD = (2, 2, 2, 2, 2, 3, 3)
        assert sum(AHEAD) == 16 and len(AHEAD) == NQ and LEAD == 2 * 16
        NORMS = [(0, TPC * n, TPC) for n in range(NCH)] + [(1, 8 * b, 8) for b in range(B)]
        BEHIND = 2

        def operand(n, w, u, g, rows):
            r = R * (n % 2)
            return QKT[n // 2][r:r + rows, w, 4 * u + g:4 * u + g + 64 * P - 63:64]

        block = ctx.enter_context(nc.Block())

        @block.sync
        def _(sp):
            for b, (r0, n) in enumerate(BLK):
                sp.dma_start(PS[0:n, b, :], pmat[r0:r0 + n, :]).then_inc(in_p, 16)
            sp.wait_ge(ct_clear, 1)
            for b, (r0, n) in enumerate(BLK):
                sp.dma_start(CT[0:n, b, :], c[:, r0:r0 + n].rearrange("b p -> p b"), allow_slow_non_contiguous=True).then_inc(in_c, 16)
            sp.dma_start(CB, c.unsqueeze(0).broadcast_to([WROWS, B, D])).then_inc(in_cb, 16)
            sp.dma_start(WL, wskew.rearrange("(p t) n -> p t n", p=WROWS)).then_inc(in_w, 16)
            for i in (0, 2, 1, 3):
                b, a = divmod(TPC * i, 8)
                sp.dma_start(X[:, TPC * i:TPC * i + TPC, :], x[b].rearrange("(p a) d -> p a d", a=8)[:, a:a + TPC, :]).then_inc(in_x[i], 16)
            sp.dma_start(BR, bskew.rearrange("(p t) -> p t", p=WROWS)).then_inc(in_br, 16)

            def staged(w, bias, dst, s_):
                sp.dma_start(dst[:, 0:2, :], w[0:2 * P, :].rearrange("(b p) n -> p b n", p=P)).then_inc(s_, 16)
                for g in range(3):
                    sp.dma_start(dst[32 * g:32 * g + 32, 2, :], w[2 * P:D, :]).then_inc(s_, 16)
                for g in range(2):
                    sp.dma_start(dst[96 + g:97 + g, 2, :], bias.rearrange("(a n) -> a n", a=1)).then_inc(s_, 16)

            staged(qkv_w, qkv_b, SWQ, in_wq)
            sp.dma_start(ADAB[:, :], ada_b.rearrange("(a n) -> a n", a=1)).then_inc(in_adab, 16)
            for b, (r0, n) in enumerate(BLK):
                sp.dma_start(ADA[0:n, b, :], ada_w[r0:r0 + n, :]).then_inc(in_ada, 16)
            sp.wait_ge(v_all, 1)
            sp.dma_start(vd.rearrange("b (p t) -> p b t", p=WROWS), VR[:, 1]).then_inc(v_out_done, 16)
            sp.wait_ge(v_out_done, 16)
            sp.wait_ge(up_clear, 1)
            for i in range(R - 1):
                at = i * (2 * R - 1 - i) // 2
                sp.dma_start(UP[i:i + 1, :, i + 1:R], vd[:, at:at + R - 1 - i].unsqueeze(0),
                             allow_slow_non_contiguous=True).then_inc(up_in, 16)
            sp.dma_start(SW2, fc2_w.rearrange("(b p) n -> p b n", p=P)).then_inc(in_w2, 16)
            sp.dma_start(SB2[:, :], fc2_b.rearrange("(a n) -> a n", a=1)).then_inc(in_w2, 16)
            staged(proj_w, proj_b, SWP, in_wp)
            staged(fc1_w, fc1_b, SW1, in_w1)
            def halves_out(n):
                for m, (f0, k) in enumerate(MT):
                    idx = NQ * n + m
                    sp.wait_ge(qk_low, idx + 1)
                    sp.dma_start(qkd[:, n, f0:f0 + k, :].rearrange("c f n -> f c n"), QS[0:k, idx % 4, :, :]).then_inc(qk_out[idx % 4], 16)
                for j in range(4):
                    sp.wait_ge(qk_out[j], 16 * len(range(j, NQ * (n + 1), 4)))

            def rows_in(dst, r, n, half, w, s_):
                sp.dma_start(dst[r:r + DH, :].rearrange("p (h c) -> p h c", h=H),
                             qkd[half, n, D * w:D * w + D, :].rearrange("(h d) c -> d h c", h=H)).then_inc(s_, 16)

            def qk_rows(n):
                for w, halves in ((0, (0, 1, 0)), (1, (0, 0, 1))):
                    for c_, half in enumerate(halves):
                        rows_in(QKT[n // 2][:, w, :], R * (n % 2) + DH * c_, n, half, w, qk_in[n])

            def v_rows(n):
                for half in range(2):
                    rows_in(VT, R * (n % 2) + DH * half, n, half, 2, v_in[n])

            def const_rows(n):
                r = R * (n % 2) + HALVES
                for w, k, src in ((0, 8, MASKQ), (1, 9, MASKK)):
                    sp.dma_start(QKT[n // 2][r:r + k, w, :].rearrange("p (h c) -> p h c", h=H),
                                 src.unsqueeze(1).broadcast_to([k, H, CH])).then_inc(att_rows[n // 2], 16)

            def max_row(n):
                sp.wait_ge(mx_half, n + 1)
                r = R * (n % 2) + MROWS
                sp.dma_start(QKT[n // 2][r:r + 1, 0, :].rearrange("p (j u) -> p j u", j=P), MR[:, n, :]).then_inc(max_in[n], 16)

            sp.wait_ge(att_const, 1)
            sp.wait_ge(fill_done, NFILL)
            const_rows(0)
            const_rows(1)
            halves_out(0)
            qk_rows(0)
            halves_out(1)
            qk_rows(1)
            sp.wait_ge(weights, 8)
            v_rows(0)
            const_rows(2)
            const_rows(3)
            v_rows(1)
            halves_out(2)
            qk_rows(2)
            max_row(0)
            halves_out(3)
            qk_rows(3)
            max_row(1)
            sp.wait_ge(vg_psum, 4)
            v_rows(2)
            max_row(2)
            sp.wait_ge(vg_psum, 8)
            v_rows(3)
            max_row(3)

            for t in range(NT):
                sp.wait_ge(y_ready, t + 1)
                sp.dma_start(out[t // 8].rearrange("(p a) d -> p a d", a=8)[:, t % 8, :], YT[:, t % 6, :]).then_inc(y_out[t % 6], 16)
            for j in range(6):
                sp.wait_ge(y_out[j], 16 * len(range(j, NT, 6)))

        @block.gpsimd
        def _(pool):
            steps = [0]

            def chain(ins):
                steps[0] += 1
                ins.then_inc(pool_step, 1)
                pool.wait_ge(pool_step, steps[0])

            pool.memset(CT[:, :, :], 0.0).then_inc(ct_clear, 1)
            chain(pool.memset(ident[:, :], 0.0))
            chain(pool.memset(below[:, :], -1.0))
            chain(pool.affine_select(out=ident[:, :], in_=ident[:, :], compare_op=ALU.not_equal, fill=1.0, base=0,
                                     pattern=[[-1, P]], channel_multiplier=1))
            chain(pool.affine_select(out=below[:, :], in_=below[:, :], compare_op=ALU.is_gt, fill=0.0, base=0,
                                     pattern=[[-1, R]], channel_multiplier=1))
            chain(pool.memset(SC32[:, :, :], 0.0))
            chain(pool.memset(ones[:, :], 1.0))
            pool.tensor_copy(G[:, R:2 * R], ident[0:R, 0:R]).then_inc(consts, 1)
            pool.wait_ge(consts, 1)
            chain(pool.tensor_scalar(TWO[:, :], ident[:, :], 2.0, None, ALU.mult))
            chain(pool.tensor_scalar(NEGI[:, :], ident[0:R, 0:R], -1.0, None, ALU.mult))
            pool.memset(UP[:, :, :], 0.0).then_inc(up_clear, 1)
            for g in range(2):
                for h in range(2):
                    chain(pool.tensor_copy(II[R * g:R * g + R, R * h:R * h + R], ident[R * g:R * g + R, R * g:R * g + R]))
            pool.memset(MOD[:, :, :, :], 0.0).then_inc(consts, 1)
            pool.wait_ge(consts, 2)
            chain(pool.memset(lowrow[:, :], 0.0))
            chain(pool.memset(lowrow[64:P, :], -1.0))
            chain(pool.affine_select(out=lowrow[96:P, :], in_=lowrow[96:P, :], compare_op=ALU.not_equal, fill=0.0, base=0,
                                     pattern=[[0, 1]], channel_multiplier=1))
            chain(pool.tensor_copy(SELV[:, :], ident[:, 0:DH]))
            for j in (DH, R, R + DH):
                chain(pool.tensor_tensor(SELV[:, :], SELV[:, :], ident[:, j:j + DH], ALU.add))
            chain(pool.memset(FOUR[:, :], FINE))
            for src, dst, n, s_ in ((SWQ, WQ, 3 * D, in_wq), (SWP, WP, D, in_wp), (SW1, W1, MLP, in_w1)):
                pool.wait_ge(s_, 96)
                chain(pool.tensor_scalar(src[:, 0:2, :], src[:, 0:2, :], FINE, None, ALU.mult))
                chain(pool.tensor_copy(dst[:, 0:2, :], src[:, 0:2, :]))
                pool.tensor_tensor(dst[:, 2:4, :], src[:, 0:2, :], dst[:, 0:2, :], ALU.subtract).then_inc(weights, 1)
                r = slice(0, 98)
                chain(pool.tensor_scalar(src[r, 2, :], src[r, 2, :], FINE, None, ALU.mult))
                chain(pool.tensor_copy(dst[r, 4, :], src[r, 2, :]))
                chain(pool.tensor_scalar(dst[r, 4, :], dst[r, 4, :], lowrow[r, :], None, ALU.mult))
                pool.tensor_tensor(dst[r, 4, :], src[r, 2, :], dst[r, 4, :], ALU.add).then_inc(weights, 1)
            pool.wait_ge(in_w2, 32)
            chain(pool.tensor_scalar(SW2, SW2, FINE, None, ALU.mult))
            chain(pool.tensor_copy(W2[:, 0], SW2))
            pool.tensor_tensor(W2[:, 1], SW2, W2[:, 0], ALU.subtract).then_inc(weights, 1)
            chain(pool.tensor_scalar(SB2[:, :], SB2[:, :], FINE, None, ALU.mult))
            chain(pool.tensor_copy(B2[:, 0], SB2[:, :]))
            pool.tensor_tensor(B2[:, 1], SB2[:, :], B2[:, 0], ALU.subtract).then_inc(weights, 1)
            chain(pool.memset(MASKK, MROW))
            for dst, value, keep in ((MASKQ, MASK[0], ALU.is_equal), (MASKK[0:8], MASK[1], ALU.not_equal)):
                chain(pool.memset(dst, value))
                sel = pool.affine_select(out=dst.rearrange("p (m c) -> p m c", m=8), in_=dst.rearrange("p (m c) -> p m c", m=8),
                                         compare_op=keep, fill=0.0, base=0, pattern=[[-1, 8], [0, 64]], channel_multiplier=1)
                chain(sel) if dst is MASKQ else sel.then_inc(att_const, 1)
            for t in range(NT):
                pool.wait_ge(proj_mul, t + 1)
                pool.tensor_tensor(X[:, t, :], X[:, t, :], YT[:, t % 6, :], ALU.add).then_inc(x_mid, 1)

        @block.tensor
        def _(pe):
            pe.wait_ge(consts, 1)
            pe.wait_ge(in_p, 48)
            for b, (r0, n) in enumerate(BLK):
                mm = pe.matmul(MISC[0:R, 0:R], PS[0:n, b, :], PS[0:n, b, :], start=(b == 0), stop=(b == 2))
            mm.then_inc(gram, 1)

            def filler(n, p_):
                f = FILL[n % 2]
                if p_ == 0 and n >= 2:
                    pe.wait_ge(fill_done, n - 1)
                if work[n] == "P'":
                    for b, (r0, k) in enumerate(BLK):
                        mm = pe.matmul(f[R * p_:R * p_ + R, r0:r0 + k], PS[0:k, b, :], ident[0:k, 0:k], start=True, stop=True)
                elif work[n] == "mod":
                    pe.wait_ge(fill_done, work.index("ada 0") + 1)
                    for b, (r0, k) in enumerate(BLK):
                        mm = pe.transpose(f[0:k, P * b:P * b + P], AD[:, 0, r0:r0 + k], ident[:, :])
                elif work[n][0] == "a":
                    if p_ == 0:
                        pe.wait_ge(in_ada, 48)
                        pe.wait_ge(in_adab, 16)
                        pe.wait_ge(silu, 1)
                    for j, v in enumerate(ADA_ROWS[int(work[n][-1])]):
                        o_, cols = f[32 * j:32 * j + 32, 0:D], slice(D * v, D * v + D)
                        if p_ < 3:
                            k = BLK[p_][1]
                            mm = pe.matmul(o_, SC32[0:k, p_, :], ADA[0:k, p_, cols], start=(p_ == 0), stop=False)
                        else:
                            mm = pe.matmul(o_, ones[0:1, 0:32], ADAB[:, cols], start=False, stop=True)
                elif work[n][1] < 3:
                    i, b = work[n]
                    if b == 0 and p_ == 0:
                        pe.wait_ge(in_x[i], 16)
                    r0, k = BLK[b]
                    mm = pe.transpose(f[0:k, P * p_:P * p_ + P], X[:, TPC * i + p_, r0:r0 + k], ident[:, :])
                else:
                    i = work[n][0]
                    if p_ == 0:
                        pe.wait_ge(fill_done, XDONE[i])
                    half, b = divmod(p_, 3)
                    r0, k = BLK[b]
                    for h in range(2):
                        c0 = CH * (i + 2 * h) + CH // 2 * half
                        mm = pe.matmul(f[R * h:R * h + R, CH // 2 * half:CH // 2 * (half + 1)], PS[0:k, b, :],
                                       XT[0:k, b, c0:c0 + CH // 2], start=(b == 0), stop=(b == 2))
                if pieces[last_piece[n]] == (n, p_):
                    mm.then_inc(fill_ready, 1)

            def gate(n):
                f = FILL[n % 2]
                pe.wait_ge(fill_done, max(n - 1, work.index("ada 1") + 1))
                g, b = divmod(n - FG, 2)
                row = 32 * g + b
                pe.matmul(f[:, 0:D], ident[0:R, row:row + 1].broadcast_to([R, P]), AD[0:R, 1, :], start=True, stop=True).then_inc(fill_ready, 1)

            def skew_matrix():
                pe.wait_ge(consts, 2)
                pe.wait_ge(up_in, 16 * (R - 1))
                for b in range(B):
                    o_ = EXPM[R * b:R * b + R, 0:R]
                    pe.matmul(o_, ident[0:R, 0:R], UP[:, b, :], start=True, stop=False)
                    mm = pe.matmul(o_, UP[:, b, :], NEGI[:, :], start=False, stop=True)
                mm.then_inc(skew_psum, 1)

            def exp_step(n):
                if n == 0:
                    pe.wait_ge(skew_ready, 2)
                pe.wait_ge(exp_sb, n + 1)
                src = YY[:, n % 2, :]
                for h in range(2):
                    cols = slice(R * h, R * h + R)
                    for b in range(B):
                        g = slice(R * b, R * b + R)
                        lhs = (XX if n < 3 else src)[g, R - R * h:2 * R - R * h]
                        mm = pe.matmul(EXPM[g, cols], lhs, src[g, cols], start=True, stop=True)
                mm.then_inc(exp_psum, 1)

            for k in range(R + LAG):
                if k < R:
                    pe.wait_ge(g_new, k + 1)
                    if k >= 2:
                        pe.wait_ge(row_ready, k - 1)
                    pe.matmul(PIV[k % 2][0:R, k:R + k + 1], ident[0:R, k:k + 1].broadcast_to([R, R]), G[:, k:R + k + 1],
                              start=True, stop=True).then_inc(piv_row, 1)
                own = pieces[max(0, PER * (k - FIRST)):max(0, PER * (k - FIRST + 1))]
                if 0 <= k - EXP_AT - 3 < NEXP:
                    exp_step(k - EXP_AT - 3)
                for n, p_ in own[:1]:
                    filler(n, p_)
                j = k - LAG
                if 0 <= j < R - 1:
                    one = ident[0:R, j:j + 1].broadcast_to([R, R])
                    pe.wait_ge(row_ready, j + 1)
                    pe.matmul(AROW[j % 2][0:R, j:R], one, ROWS[:, j % 4, j:R], start=True, stop=False)
                    pe.wait_ge(a_new, j + 1)
                    pe.matmul(AROW[j % 2][0:R, j:R], NEGI[:, j:j + 1].broadcast_to([R, R]), A[:, j:R], start=False, stop=False)
                    pe.wait_ge(a_sign, j + 1)
                    pe.matmul(AROW[j % 2][0:R, j:R], SG[:, j:j + 1].broadcast_to([R, R]), A[:, j:R],
                              start=False, stop=True).then_inc(a_row, 1)
                for n, p_ in own[1:]:
                    filler(n, p_)
                if k == EXP_AT:
                    skew_matrix()

            pe.wait_ge(basis, 2)
            pe.wait_ge(exp_sb, NEXP + 1)
            last = YY[:, NEXP % 2, :]
            for b in range(B):
                g = slice(R * b, R * b + R)
                mm = pe.matmul(EXPM[g, 0:R], last[g, R:2 * R], V2[g, :], start=True, stop=True)
            mm.then_inc(rot_psum, 1)
            pe.wait_ge(rot_sb, 1)
            for b in range(B):
                g = slice(R * b, R * b + R)
                mm = pe.matmul(MISC[g, 0:R], T1[g, :], V2[g, :], start=True, stop=True)
            mm.then_inc(rot_psum, 1)
            pe.wait_ge(rot_sb, 2)
            for b in range(B):
                g = slice(R * b, R * b + R)
                mm = pe.matmul(PIV[0][g, 0:D], NTs[g, :], PT2[g, :], start=True, stop=True)
            mm.then_inc(rot_psum, 1)
            pe.wait_ge(rot_sb, 3)
            pe.wait_ge(fill_done, FG)

            def delta(t):
                if t >= 2:
                    pe.wait_ge(x_rot, t - 1)
                b, a = divmod(t, 8)
                g = slice(R * b, R * b + R)
                pe.matmul(FILL[t % 2][:, 0:D], ZT[g, P * a:P * a + P], ROT[g, :], start=True, stop=True).then_inc(delta_ready, 1)

            for t in range(2 * TPC):
                delta(t)
            pe.wait_ge(x_rot, 2 * TPC)
            for n in range(FG, NFILL):
                gate(n)

            def turn(n):
                attended = NCH <= n < 2 * NCH
                if attended:
                    pe.wait_ge(o_norm, 8 * ((n - NCH) // 2 + 1))
                else:
                    pe.wait_ge(xn_ready, modulated(n) + 1)
                for b, (r0, k) in enumerate(BLK):
                    idx = 3 * n + b
                    if idx >= 2:
                        pe.wait_ge(split_done if NCH <= (idx - 2) // 3 < 2 * NCH else cast_done, idx - 1)
                    f = TRB[idx % 2]
                    for j in range(TPC):
                        cols = slice(P * j, P * j + P)
                        rows = 96 if b == 2 else P
                        if not attended:
                            mm = pe.transpose(f[0:rows, cols], XN[:, n % 2, j, r0:r0 + rows], ident[:, :])
                            continue
                        at = D * (TPC * (n - NCH) + j) + r0
                        if b < 2:
                            mm = pe.transpose(f[:, cols], stage[:, at:at + P], ident[:, :])
                        else:
                            for g in range(3):
                                mm = pe.matmul(f[32 * g:32 * g + 32, cols], stage[:, at:at + 32], ident[:, :], start=True, stop=True)
                    mm.then_inc(tr_ready, 1)

            def maxima(s_):
                n, u = divmod(s_, 16)
                if u == 0:
                    pe.wait_ge(qk_in[n], 96)
                    pe.wait_ge(att_rows[n // 2], 64)
                if s_ == 0:
                    pe.wait_ge(x_rot, NT)
                if s_ >= 2:
                    pe.wait_ge(mx_used, s_ - 1)
                for g in range(4):
                    mm = pe.matmul(MXB[s_ % 2][:, P * g:P * g + P], operand(n, 0, u, g, MROWS), operand(n, 1, u, g, MROWS),
                                   start=True, stop=True)
                mm.then_inc(mx_ready, 1)

            def qkv(n):
                pe.wait_ge(split_done, 3 * n + 3)
                if n == 0:
                    pe.wait_ge(weights, 2)
                for m, (f0, k) in enumerate(MT):
                    if m == TURN_AT and n + 1 < NCH:
                        turn(n + 1)
                    idx = NQ * n + m
                    if idx >= 3:
                        pe.wait_ge(qk_low, idx - 2)
                    for p_, (a_, w_, r) in enumerate(PARTS):
                        mm = pe.matmul(QB[idx % 3][0:k, :], WQ[0:r, w_, f0:f0 + k], HT[0:r, n % 2, a_, :], start=(p_ == 0), stop=(p_ == 6))
                    mm.then_inc(qk_ready, 1)
                    for s_ in range(AHEAD[m] if n >= 2 else 0):
                        maxima(16 * (n - 2) + sum(AHEAD[:m]) + s_)
                    if m < TPC and n + 2 < NCH:
                        if n == 0 and m == 0:
                            pe.wait_ge(fill_done, NFILL)
                        delta(TPC * (n + 2) + m)

            turn(0)
            for n in range(NCH):
                qkv(n)

            def scores(s_):
                n, u = divmod(s_, 16)
                if u == 0:
                    pe.wait_ge(max_in[n], 16)
                if s_ >= 2:
                    pe.wait_ge(exp_done, s_ - 1)
                for g in range(4):
                    mm = pe.matmul(SB[s_ % 2][:, P * g:P * g + P], operand(n, 1, u, g, MROWS + 1), operand(n, 0, u, g, MROWS + 1),
                                   start=True, stop=True)
                mm.then_inc(s_ready, 1)

            def v_groups(w):
                n, q = divmod(w, 4)
                r = R * (n % 2)
                if q == 0:
                    pe.wait_ge(v_in[n], 32)
                if w:
                    pe.wait_ge(vg_ready, w)
                for g in range(16):
                    mm = pe.matmul(VB[:, DH * g:DH * g + DH], VT[r:r + 2 * DH, 16 * q + g:16 * q + g + 64 * P - 63:64], SELV[r:r + 2 * DH, :],
                                   start=True, stop=True)
                mm.then_inc(vg_psum, 1)

            def values(s_):
                w, q = divmod(s_, 4)
                pe.wait_ge(exp_done, s_ + 1)
                if q == 0:
                    pe.wait_ge(vg_ready, w + 1)
                    if w >= 2:
                        pe.wait_ge(ot_ready, w - 1)
                for g in range(4):
                    mm = pe.matmul(PO[w % 2][32 * g:32 * g + 32, P * q:P * q + P], VG[:, w % 2, 4 * q + g, :],
                                   E[:, s_ % 3, P * g:P * g + P], start=True, stop=True)
                mm.then_inc(pv_ready, 1)

            def turn_values(w):
                pe.wait_ge(ot_ready, w + 1)
                if w:
                    pe.wait_ge(o_norm, w)
                for q in range(4):
                    mm = pe.transpose(OB[:, P * q:P * q + P], OT[w % 2][:, P * q:P * q + P], ident[:, :])
                mm.then_inc(o_turned, 1)

            pe.wait_ge(cast_done, 3 * NCH)
            pe.wait_ge(qk_low, NQ * NCH)
            v_groups(0)
            for s_ in range(LEAD, UNITS + LEAD + 4):
                st = s_ - LEAD
                if s_ < UNITS:
                    maxima(s_)
                if 0 <= st < UNITS:
                    scores(st)
                if 0 <= st - BEHIND < UNITS:
                    values(st - BEHIND)
                    if st % 4 == 2 and st // 4 + 1 < UNITS // 4:
                        v_groups(st // 4 + 1)
                if st >= 7 and st % 4 == 3:
                    turn_values(st // 4 - 1)

            def project(n):
                pe.wait_ge(split_done, 3 * n + 3)
                if n == NCH:
                    pe.wait_ge(weights, 4)
                for j in range(TPC):
                    t = TPC * (n - NCH) + j
                    if t >= 3:
                        pe.wait_ge(proj_mul, t - 2)
                    for p_, (a_, w_, r) in enumerate(PARTS):
                        mm = pe.matmul(QB[t % 3][:, 0:D], HT[0:r, n % 2, a_, P * j:P * j + P], WP[0:r, w_, :], start=(p_ == 0), stop=(p_ == 6))
                    mm.then_inc(proj_ready, 1)

            turn(NCH)
            for n in range(NCH, 2 * NCH):
                if n + 1 < 2 * NCH:
                    turn(n + 1)
                project(n)
            turn(2 * NCH)

            def fc1(n):
                pe.wait_ge(split_done, 3 * n + 3)
                if n == 2 * NCH:
                    pe.wait_ge(weights, 6)
                for m in range(NF):
                    if m == TURN1_AT and n + 1 < 3 * NCH:
                        turn(n + 1)
                    idx = NF * (n - 2 * NCH) + m
                    if idx >= 3:
                        pe.wait_ge(gelu_sb, idx - 2)
                    for p_, (a_, w_, r) in enumerate(PARTS):
                        mm = pe.matmul(FB[idx % 3], W1[0:r, w_, P * m:P * m + P], HT[0:r, n % 2, a_, :], start=(p_ == 0), stop=(p_ == 6))
                    mm.then_inc(fc1_ready, 1)

            def fc2(n):
                c_ = n - 2 * NCH
                pe.wait_ge(g_low, NF * (c_ + 1))
                if c_ == 0:
                    pe.wait_ge(weights, 8)
                g = GT[c_ % 2]
                for j in range(TPC):
                    t = TPC * c_ + j
                    if t >= 2:
                        pe.wait_ge(y_mul, t - 1)
                    cols = slice(P * j, P * j + P)
                    for half in range(2):
                        pe.matmul(YB[t % 2][:, 0:D], FOUR[:, :], B2[:, half, :], start=(half == 0), stop=False)
                    for f in range(NF):
                        for a_, w_ in ((0, 0), (1, 0), (0, 1)):
                            mm = pe.matmul(YB[t % 2][:, 0:D], g[:, a_, f, cols], W2[:, w_, f, :], start=False, stop=(f == NF - 1 and w_ == 1))
                    mm.then_inc(fc2_ready, 1)

            for n in range(2 * NCH, 3 * NCH):
                fc1(n)
                if n > 2 * NCH:
                    fc2(n - 1)
            fc2(3 * NCH - 1)

        @block.scalar
        def _(act):
            act.wait_ge(in_c, 48)
            act.activation(SC[:, 0], CT[:, :, :], ACT.Exp, scale=-1.0).then_inc(silu_e, 1)

            act.wait_ge(in_cb, 16)
            act.activation(SCB[:, 0], CB, ACT.Exp, scale=-1.0).then_inc(cb_e, 1)
            act.wait_ge(cb_e, 1)
            act.activation(SCB[:, 1], SCB[:, 0], ACT.Copy, bias=1.0).then_inc(cb_e, 1)

            def fill_out(n):
                act.wait_ge(fill_ready, n + 1)
                f = FILL[n % 2]
                if n >= FG:
                    g, b = divmod(n - FG, 2)
                    cp = act.mul(GATE[:, g, b, :], f[:, 0:D], 1.0 / (FINE * FINE))
                elif work[n] == "P'":
                    cp = act.copy(PT2[:, :], f[:, 0:D])
                elif work[n] == "mod":
                    act.wait_ge(consts, 2)
                    fv = f[:, 0:3 * P].rearrange("p (m v b) -> p v m b", m=3, v=4)[:, :, :, 0:B]
                    for q in range(2):
                        cp = act.activation(MOD[:, q:4:2, 0:2, :], fv[:, q:4:2, 0:2, :], ACT.Copy, scale=FINE, bias=FINE * q)
                        for rep in range(3):
                            cp = act.activation(MOD[32 * rep:32 * rep + 32, q:4:2, 2, :], fv[0:32, q:4:2, 2, :], ACT.Copy, scale=FINE, bias=FINE * q)
                            if rep < 2 or q == 0:
                                cp.then_inc(mod_part, 1)
                elif work[n][0] == "a":
                    g = int(work[n][-1])
                    rows = 32 * len(ADA_ROWS[g])
                    cp = act.copy(AD[0:rows, g, :], f[0:rows, 0:D])
                else:
                    i, b = work[n]
                    if b < 3:
                        k = BLK[b][1]
                        cp = act.copy(XT[0:k, b, CH * i:CH * i + CH], f[0:k, :])
                    else:
                        act.wait_ge(v_all, 1)
                        cp = act.copy(ZT[:, CH * i:CH * i + CH], f[:, :])
                cp.then_inc(fill_done, 1)

            for k in range(R + LAG + 1):
                if k < R - 1:
                    act.wait_ge(piv_inv, k + 1)
                    act.activation(RHO[:, k:k + 1], RI[:, k:k + 1], ACT.Sqrt, scale=1.0).then_inc(rho_ready, 1)
                    act.wait_ge(rho_ready, k + 1)
                    act.wait_ge(g_new, k + 2)
                    if k >= 4:
                        act.wait_ge(a_new, k - 2)
                    act.activation(ROWS[:, k % 4, k:R], PIV[k % 2][0:R, k:R], ACT.Copy, scale=RHO[:, k:k + 1]).then_inc(row_ready, 1)
                for n, i in last_piece.items():
                    if FIRST + i // PER == k - 1:
                        fill_out(n)
                if k == EXP_AT:
                    act.wait_ge(skew_psum, 1)
                    for h in range(2):
                        act.mul(XX[:, R * h:R * h + R], EXPM[:, 0:R], (1 - 2 * h) * 2.0 ** -SQUARINGS).then_inc(skew_ready, 1)
            act.wait_ge(diag, 2)
            act.activation(dg[:, 2:3], dg[:, 0:1], ACT.Sqrt, scale=1.0).then_inc(root, 1)

            def norm_root(q):
                l, t0, k = NORMS[q]
                act.wait_ge(stats, q + 1)
                act.activation(ST[:, l, 1, t0:t0 + k], ST[:, l, 0, t0:t0 + k], ACT.Sqrt).then_inc(root2, 1)

            def turn_out(n, l):
                if 2 <= n < NCH:
                    act.wait_ge(qk_ready, NQ * (n - 1))
                elif n < NCH + 2 and l is None:
                    act.wait_ge(o_turned, UNITS // 4)
                elif NCH < n < 2 * NCH + 2:
                    act.wait_ge(proj_ready, TPC * (n - NCH - 1))
                elif n >= 2 * NCH + 2:
                    act.wait_ge(fc1_ready, NF * (n - 2 * NCH - 1))
                for b in range(3):
                    idx = 3 * n + b
                    act.wait_ge(tr_ready, idx + 1)
                    rows = 96 if b == 2 else P
                    batch = (n % NCH) // 2
                    src, high = TRB[idx % 2][0:rows, :], HT[0:rows, n % 2, 4 if b == 2 else b, :]
                    if l == 0:
                        src = src.rearrange("p (a m v) -> p a m v", a=TPC, m=8)
                        high = high.rearrange("p (m a v) -> p a m v", a=TPC, m=8)
                    if l is None:
                        act.mul(high, src, FINE).then_inc(cast_done, 1)
                        continue
                    if idx >= 2:
                        act.wait_ge(split_done, idx - 1)
                    full = T32[0:rows, idx % 2, :]
                    if l == 0:
                        full = full.rearrange("p (m a v) -> p a m v", a=TPC, m=8)
                    for dst, s_ in ((full, t32_ready), (high, cast_done)):
                        act.activation(dst, src, ACT.Identity, scale=MOD[0:rows, 2 * l + 1, b, batch:batch + 1],
                                       bias=MOD[0:rows, 2 * l, b, batch:batch + 1]).then_inc(s_, 1)

            def qkv_out(n):
                for m, (f0, k) in enumerate(MT):
                    if m == TURN_AT and n + 1 < NCH:
                        turn_out(n + 1, 0)
                    idx = NQ * n + m
                    act.wait_ge(qk_ready, idx + 1)
                    if idx >= 4:
                        act.wait_ge(qk_out[idx % 4], 16 * (idx // 4))
                    act.mul(QS[0:k, idx % 4, 0, :], QB[idx % 3][0:k, :], QSCALE / (FINE * FINE)).then_inc(qk_high, 1)

            norm_root(0)
            norm_root(1)
            for n in range(FG, NFILL):
                fill_out(n)
            turn_out(0, 0)
            for n in range(NCH):
                qkv_out(n)
                if n + 2 < NCH:
                    norm_root(n + 2)

            def exponentials(s_):
                act.wait_ge(s_ready, s_ + 1)
                if s_ >= 3:
                    act.wait_ge(pv_ready, s_ - 2)
                act.activation(E[:, s_ % 3, :], SB[s_ % 2], ACT.Exp, scale=DH ** -0.5 / (QSCALE * QSCALE)).then_inc(exp_done, 1)

            def v_out(w):
                act.wait_ge(vg_psum, w + 1)
                if w == 0:
                    act.wait_ge(vg_clear, 2)
                if w >= 2:
                    act.wait_ge(pv_ready, 4 * w - 4)
                act.mul(VG[:, w % 2, :, 0:DH], VB[:, 0:16 * DH].rearrange("p (g d) -> p g d", g=16), 1.0 / QSCALE).then_inc(vg_ready, 1)

            def values_out(w):
                act.wait_ge(pv_ready, 4 * w + 4)
                if w >= 2:
                    act.wait_ge(o_turned, w - 1)
                act.copy(OT[w % 2], PO[w % 2]).then_inc(ot_ready, 1)

            v_out(0)
            for st in range(UNITS + 4):
                if st < UNITS:
                    exponentials(st)
                if st >= BEHIND and st % 4 == 2 and st // 4 + 1 < UNITS // 4:
                    v_out(st // 4 + 1)
                if st >= 6 and st % 4 == 2:
                    values_out((st - 6) // 4)

            turn_out(NCH, None)
            for n in range(NCH, 2 * NCH):
                if n + 1 < 2 * NCH:
                    turn_out(n + 1, None)
            norm_root(NCH)
            turn_out(2 * NCH, 1)
            norm_root(NCH + 1)

            def gelu(n):
                for m in range(NF):
                    if m == TURN1_AT and n + 1 < 3 * NCH:
                        turn_out(n + 1, 1)
                    idx = NF * (n - 2 * NCH) + m
                    act.wait_ge(fc1_ready, idx + 1)
                    if idx >= 2:
                        act.wait_ge(g_low, idx - 1)
                    act.activation(G32[:, idx % 2, :], FB[idx % 3], ACT.Gelu, scale=1.0 / (FINE * FINE)).then_inc(gelu_sb, 1)

            for n in range(2 * NCH, 3 * NCH):
                gelu(n)

        @block.vector
        def _(dve):
            dve.wait_ge(gram, 1)
            dve.wait_ge(consts, 1)
            dve.tensor_copy(G[:, 0:R], MISC[0:R, 0:R]).then_inc(g_new, 1)
            dve.tensor_copy(A[:, :], PS[0:R, 0, :]).then_inc(a_new, 1)
            dve.wait_ge(g_new, 1)
            dve.wait_ge(a_new, 1)

            def silu_cond():
                dve.wait_ge(silu_e, 1)
                dve.tensor_scalar(SC[:, 1], SC[:, 0], 1.0, None, ALU.add).then_inc(silu_e, 1)
                dve.wait_ge(silu_e, 2)
                dve.reciprocal(SC[:, 2], SC[:, 1]).then_inc(silu_e, 1)
                dve.wait_ge(silu_e, 3)
                dve.tensor_tensor(SC32[:, :, 0:B], SC[:, 2], CT[:, :, :], ALU.mult).then_inc(silu, 1)

            def silu_rows():
                dve.wait_ge(cb_e, 2)
                dve.reciprocal(SCB[:, 2], SCB[:, 1]).then_inc(cb_e, 1)
                dve.wait_ge(cb_e, 3)
                dve.tensor_tensor(SCB[:, 2], SCB[:, 2], CB, ALU.mult).then_inc(cb_done, 1)

            def skew_entries(t):
                if t == 0:
                    dve.wait_ge(in_w, 16)
                    dve.wait_ge(cb_done, 1)
                for b in range(B):
                    n = B * t + b
                    if n >= 4:
                        dve.wait_ge(v_sum, n - 3)
                    dve.tensor_tensor_reduce(JUNK[:, n % 4, :], WL[:, t, :], SCB[:, 2, b, :], 1.0, 0.0, ALU.mult, ALU.add,
                                             VR[:, 0, b, t:t + 1]).then_inc(v_sum, 1)

            def sign(j):
                dve.scalar_tensor_tensor(out=SG[:, j:j + 1], in0=A[:, j:j + 1], scalar=0.0, in1=TWO[0:R, j:j + 1],
                                         op0=ALU.is_ge, op1=ALU.mult).then_inc(a_sign, 1)

            def exp_out(n):
                dst = YY[:, (n + 1) % 2, :]
                if n == -1:
                    dve.wait_ge(skew_ready, 2)
                    op = dve.scalar_tensor_tensor(out=dst, in0=XX[:, :], scalar=0.25, in1=II[:, :], op0=ALU.mult, op1=ALU.add)
                else:
                    dve.wait_ge(exp_psum, n + 1)
                    if n < 2:
                        op = dve.scalar_tensor_tensor(out=dst, in0=EXPM[:, 0:2 * R], scalar=1.0 / (3 - n), in1=II[:, :], op0=ALU.mult, op1=ALU.add)
                    elif n == 2:
                        op = dve.tensor_copy(dst, EXPM[:, 0:2 * R])
                    else:
                        dve.wait_ge(exp_sb, n + 1)
                        op = dve.scalar_tensor_tensor(out=dst, in0=YY[:, n % 2, :], scalar=2.0, in1=EXPM[:, 0:2 * R], op0=ALU.mult, op1=ALU.add)
                op.then_inc(exp_sb, 1)

            dve.wait_ge(consts, 2)
            sign(0)
            for k in range(R + LAG):
                j = k - LAG
                if k < R:
                    dve.wait_ge(piv_row, k + 1)
                    dve.reciprocal(RI[:, k:k + 1], PIV[k % 2][0:R, k:k + 1]).then_inc(piv_inv, 1)
                if k < R - 1:
                    dve.wait_ge(piv_inv, k + 1)
                    dve.tensor_scalar(CG[:, k:k + 1], G[:, k:k + 1], RI[:, k:k + 1], below[:, k:k + 1], ALU.mult, ALU.mult).then_inc(gcoef, 1)
                    dve.wait_ge(gcoef, k + 1)
                    dve.scalar_tensor_tensor(out=G[:, k + 1:R + k + 1], in0=PIV[k % 2][0:R, k + 1:R + k + 1], scalar=CG[:, k:k + 1],
                                             in1=G[:, k + 1:R + k + 1], op0=ALU.mult, op1=ALU.add).then_inc(g_new, 1)
                if 0 <= j < R - 1:
                    dve.wait_ge(a_row, j + 1)
                    dve.reciprocal(RA[:, j:j + 1], AROW[j % 2][0:R, j:j + 1]).then_inc(a_piv, 1)
                    dve.wait_ge(a_piv, j + 1)
                    dve.tensor_scalar(CA[:, j:j + 1], A[:, j:j + 1], RA[:, j:j + 1], below[:, j:j + 1], ALU.mult, ALU.mult).then_inc(acoef, 1)
                    dve.wait_ge(acoef, j + 1)
                    dve.scalar_tensor_tensor(out=A[:, j + 1:R], in0=AROW[j % 2][0:R, j + 1:R], scalar=CA[:, j:j + 1],
                                             in1=A[:, j + 1:R], op0=ALU.mult, op1=ALU.add).then_inc(a_new, 1)
                    dve.wait_ge(a_new, j + 2)
                    sign(j + 1)
                if k == 2:
                    silu_cond()
                    silu_rows()
                if V_AT <= k < V_AT + WTILES:
                    skew_entries(k - V_AT)
                if k == V_AT + WTILES:
                    dve.wait_ge(v_sum, B * WTILES)
                    dve.wait_ge(in_br, 16)
                    dve.tensor_tensor(VR[:, 1], VR[:, 0], BR.unsqueeze(1).broadcast_to([WROWS, B, WTILES]), ALU.add).then_inc(v_all, 1)
                if -1 <= k - EXP_AT - 2 < NEXP:
                    exp_out(k - EXP_AT - 2)
            dve.wait_ge(a_sign, R)
            dve.wait_ge(piv_inv, R)
            for n, src in ((0, RI), (1, SG)):
                dve.tensor_tensor_reduce(DJ[:, n, :], src[:, :], ident[0:R, 0:R], 1.0, 0.0, ALU.mult, ALU.add, dg[:, n:n + 1]).then_inc(diag, 1)
            dve.wait_ge(root, 1)
            dve.wait_ge(diag, 2)
            dve.reciprocal(dg[:, 3:4], dg[:, 2:3]).then_inc(root, 1)
            dve.wait_ge(root, 2)
            dve.tensor_scalar(dg[:, 4:5], dg[:, 3:4], dg[:, 0:1], dg[:, 2:3], ALU.mult, ALU.add).then_inc(root, 1)
            dve.tensor_scalar(dg[:, 5:6], dg[:, 1:2], 0.5, 0.5, ALU.mult, ALU.subtract).then_inc(root, 1)
            dve.wait_ge(root, 4)
            dve.wait_ge(g_new, R)
            for g in range(2):
                dve.tensor_scalar(V2[R * g:R * g + R, :], G[:, R:2 * R], dg[:, 4:5], dg[:, 5:6], ALU.mult, ALU.mult).then_inc(basis, 1)
            dve.wait_ge(rot_psum, 1)
            dve.tensor_copy(T1[:, :], EXPM[:, 0:R]).then_inc(rot_sb, 1)
            dve.wait_ge(rot_psum, 2)
            dve.tensor_copy(NTs[:, :], MISC[:, 0:R]).then_inc(rot_sb, 1)
            dve.wait_ge(rot_psum, 3)
            dve.tensor_copy(ROT[:, :], PIV[0][:, 0:D]).then_inc(rot_sb, 1)
            def stat(l, t):
                idx = NT * l + t
                if t >= 2 or l:
                    dve.wait_ge(bn_s, 2 * idx - 2)
                dve.bn_stats(BN[:, t % 2, :], X[:, t, :]).then_inc(bn_s, 1)
                dve.wait_ge(bn_s, 2 * idx + 1)
                dve.bn_aggr(MV[:, l, t, :], BN[:, t % 2, :]).then_inc(bn_s, 1)

            def norm_scales(q):
                l, t0, k = NORMS[q]
                s_ = ST[:, l, :, t0:t0 + k]
                dve.wait_ge(bn_s, 2 * (NT * l + t0 + k))
                dve.tensor_scalar(s_[:, 0, :], MV[:, l, t0:t0 + k, 1], EPS, None, ALU.add).then_inc(stats, 1)
                dve.wait_ge(root2, q + 1)
                dve.wait_ge(stats, q + 1)
                dve.reciprocal(s_[:, 2, :], s_[:, 1, :]).then_inc(scales, 1)
                dve.wait_ge(scales, 5 * q + 1)
                dve.tensor_tensor(s_[:, 3, :], s_[:, 2, :], s_[:, 2, :], ALU.mult).then_inc(scales, 1)
                dve.wait_ge(scales, 5 * q + 2)
                dve.tensor_tensor(s_[:, 4, :], s_[:, 3, :], s_[:, 0, :], ALU.mult).then_inc(scales, 1)
                dve.wait_ge(scales, 5 * q + 3)
                dve.tensor_scalar(s_[:, 5, :], s_[:, 4, :], -0.5, 1.5, ALU.mult, ALU.add).then_inc(scales, 1)
                dve.wait_ge(scales, 5 * q + 4)
                dve.tensor_tensor(s_[:, 6, :], s_[:, 5, :], s_[:, 2, :], ALU.mult).then_inc(scales, 1)
                dve.wait_ge(scales, 5 * q + 5)

            def source(n, l):
                if n >= 2:
                    dve.wait_ge(tr_ready, 3 * n - 3)
                for j in range(TPC):
                    t = TPC * (n % NCH) + j
                    dve.tensor_scalar(XN[:, n % 2, j, 0:D], X[:, t, :], MV[:, l, t, 0:1], ST[:, l, 6, t:t + 1],
                                      ALU.subtract, ALU.mult).then_inc(xn_main, 1)
                dve.wait_ge(xn_main, TPC * (modulated(n) + 1))
                dve.tensor_copy(XN[:, n % 2, :, D:DX].rearrange("p t (a c) -> p t a c", a=2),
                                XN[:, n % 2, :, D - 32:D].unsqueeze(2).broadcast_to([P, TPC, 2, 32])).then_inc(xn_ready, 1)

            def split(n):
                for b in range(3):
                    idx = 3 * n + b
                    dve.wait_ge(cast_done, idx + 1)
                    rows = slice(32, 64) if b == 2 else slice(0, P)
                    low = HT[rows, n % 2, 4 if b == 2 else 2 + b, :]
                    high = HT[rows, n % 2, 4 if b == 2 else b, :]
                    if NCH <= n < 2 * NCH:
                        dve.scalar_tensor_tensor(out=low, in0=TRB[idx % 2][rows, :], scalar=FINE, in1=high,
                                                 op0=ALU.mult, op1=ALU.subtract).then_inc(split_done, 1)
                    else:
                        dve.wait_ge(t32_ready, 3 * modulated(n) + b + 1)
                        dve.tensor_tensor(low, T32[rows, idx % 2, :], high, ALU.subtract).then_inc(split_done, 1)

            def maximum(s_):
                n, u = divmod(s_, 16)
                dve.wait_ge(mx_ready, s_ + 1)
                dve.tensor_reduce(MX[:, n, 4 * u:4 * u + 4], MXB[s_ % 2].rearrange("p (g c) -> p g c", g=4), AX.X, ALU.max,
                                  negate=True).then_inc(mx_used, 1)
                if u == 15:
                    dve.wait_ge(mx_used, s_ + 1)
                    dve.tensor_scalar(MR[:, n, :], MX[:, n, :], 1.0 / MROW, None, ALU.mult).then_inc(mx_half, 1)

            def ones_rows(n):
                for a_ in range(2):
                    dve.memset(HT[96:P, a_, 4, :], FINE).then_inc(ht_ones, 1)
                dve.wait_ge(ht_ones, 2 * n + 2)

            def rotated(t):
                dve.wait_ge(delta_ready, t + 1)
                dve.tensor_tensor(X[:, t, :], FILL[t % 2][:, 0:D], X[:, t, :], ALU.add).then_inc(x_rot, 1)
                if t >= 1:
                    dve.wait_ge(x_rot, t)
                    if t % TPC:
                        stat(0, t - 1)
                if t % TPC == TPC - 1:
                    dve.wait_ge(x_rot, t + 1)
                    stat(0, t)

            for t in range(2 * TPC):
                rotated(t)
                if t % TPC == TPC - 1:
                    norm_scales(t // TPC)
            dve.wait_ge(fill_done, FG)
            ones_rows(0)
            source(0, 0)
            source(1, 0)
            split(0)
            for n in range(NCH):
                for m, (f0, k) in enumerate(MT):
                    if m == TURN_AT and n + 1 < NCH:
                        split(n + 1)
                    idx = NQ * n + m
                    dve.wait_ge(qk_high, idx + 1)
                    dve.scalar_tensor_tensor(out=QS[0:k, idx % 4, 1, :], in0=QB[idx % 3][0:k, :], scalar=QSCALE / (FINE * FINE),
                                             in1=QS[0:k, idx % 4, 0, :], op0=ALU.mult, op1=ALU.subtract).then_inc(qk_low, 1)
                    for s_ in range(AHEAD[m] if n >= 2 else 0):
                        maximum(16 * (n - 2) + sum(AHEAD[:m]) + s_)
                    if m < TPC and n + 2 < NCH:
                        rotated(TPC * (n + 2) + m)
                if n + 2 < NCH:
                    norm_scales(n + 2)
                    source(n + 2, 0)
            dve.wait_ge(split_done, 3 * NCH)
            dve.memset(VG[:, :, :, :], 0.0).then_inc(vg_clear, 1)
            dve.wait_ge(vg_clear, 1)
            dve.memset(VG[:, :, :, DH:DH + 1], 1.0).then_inc(vg_clear, 1)

            def normalise(w):
                n, q = divmod(w, 4)
                dve.wait_ge(o_turned, w + 1)
                if w == 0:
                    dve.wait_ge(weights, 8)
                if w >= 2:
                    dve.wait_ge(o_norm, w - 1)
                po = OB.rearrange("p (g d) -> p g d", g=16)
                dve.reciprocal(RD[:, w % 2, :], po[:, :, DH]).then_inc(o_sum, 1)
                dve.wait_ge(o_sum, w + 1)
                dve.tensor_tensor(AO[:, n // 2, :, :, 4 * (n % 2) + q, :],
                                  po[:, :, 0:DH].rearrange("p (a e) d -> p a e d", e=2),
                                  RD[:, w % 2, :].rearrange("p (a e) -> p a e", e=2).unsqueeze(3).broadcast_to([P, 8, 2, DH]),
                                  ALU.mult).then_inc(o_norm, 1)

            for s_ in range(LEAD, UNITS + LEAD + 5):
                if s_ < UNITS:
                    maximum(s_)
                st = s_ - LEAD
                if st >= 8 and st % 4 == 0:
                    normalise(st // 4 - 2)
            dve.wait_ge(o_norm, UNITS // 4)
            split(NCH)
            for n in range(NCH, 2 * NCH):
                if n + 1 < 2 * NCH:
                    split(n + 1)
                for j in range(TPC):
                    t = TPC * (n - NCH) + j
                    dve.wait_ge(proj_ready, t + 1)
                    if t >= 6:
                        dve.wait_ge(x_mid, t - 5)
                    dve.tensor_tensor(YT[:, t % 6, :], QB[t % 3][:, 0:D], GATE[:, 0, t // 8, :], ALU.mult).then_inc(proj_mul, 1)
                    if t >= 3:
                        dve.wait_ge(x_mid, t - 2)
                        stat(1, t - 3)
                    if t == 3 * TPC + 1:
                        norm_scales(NCH)
                        source(2 * NCH, 1)
            split(2 * NCH)
            for t in range(NT - 3, NT):
                dve.wait_ge(x_mid, t + 1)
                stat(1, t)
            source(2 * NCH + 1, 1)
            norm_scales(NCH + 1)

            def gelu_split(n):
                c_ = n - 2 * NCH
                for m in range(NF):
                    if m == TURN1_AT and n + 1 < 3 * NCH:
                        split(n + 1)
                    idx = NF * c_ + m
                    dve.wait_ge(gelu_sb, idx + 1)
                    if m == 0 and c_ >= 2:
                        dve.wait_ge(fc2_ready, TPC * (c_ - 1))
                    dve.tensor_scalar(GT[c_ % 2][:, 0, m, :], G32[:, idx % 2, :], FINE, None, ALU.mult).then_inc(g_high, 1)
                    dve.wait_ge(g_high, idx + 1)
                    dve.scalar_tensor_tensor(out=GT[c_ % 2][:, 1, m, :], in0=G32[:, idx % 2, :], scalar=FINE,
                                             in1=GT[c_ % 2][:, 0, m, :], op0=ALU.mult, op1=ALU.subtract).then_inc(g_low, 1)

            def result(n):
                for j in range(TPC):
                    t = TPC * (n - 2 * NCH) + j
                    dve.wait_ge(fc2_ready, t + 1)
                    if t >= 6:
                        dve.wait_ge(y_out[t % 6], 16 * (t // 6))
                    dve.tensor_tensor(YT[:, t % 6, :], YB[t % 2][:, 0:D], GATE[:, 1, t // 8, :], ALU.mult).then_inc(y_mul, 1)
                    dve.wait_ge(y_mul, t + 1)
                    dve.tensor_tensor(YT[:, t % 6, :], YT[:, t % 6, :], X[:, t, :], ALU.add).then_inc(y_ready, 1)

            for n in range(2 * NCH, 3 * NCH):
                gelu_split(n)
                if n + 2 < 3 * NCH:
                    source(n + 2, 1)
                if n > 2 * NCH:
                    result(n - 1)
            result(3 * NCH - 1)


_INS = ["x", "cond_1152", "L0_cond_P", "L0_cond_W", "L0_cond_b", "L1_cond_qkv_w", "L1_cond_qkv_b", "L1_cond_proj_w",
        "L1_cond_proj_b", "L1_cond_fc1_w", "L1_cond_fc1_b", "L1_cond_fc2_w", "L1_cond_fc2_b", "L1_cond_ada_w", "L1_cond_ada_b"]


def kernel(**inputs):
    import numpy as _np
    import concourse.bacc as _bacc
    from concourse import mybir as _mybir
    from concourse.bass_utils import run_bass_kernel_spmd as _run

    nc = _bacc.Bacc("TRN2", target_bir_lowering=False, num_devices=1)
    arrays, args = {}, []
    for name in _INS:
        a = _np.ascontiguousarray(inputs[name])
        arrays[f"in_{name}_dram"] = a
        args.append(nc.dram_tensor(f"in_{name}_dram", a.shape, _mybir.dt.from_np(a.dtype), kind="ExternalInput").ap())
    args.append(nc.dram_tensor("out_0_dram", (2, 1024, 288), _mybir.dt.float32, kind="ExternalOutput").ap())
    build(nc, *args)
    r = _run(nc, [arrays], core_ids=[0])
    return r.results[0]["out_0_dram"]
```
